# Optimizing a Trainium2 kernel written in Bass

```python
import numpy as np
import jax
import jax.numpy as jnp

def _softmax(x, axis=-1):
    return jax.nn.softmax(x, axis=axis)

def _gelu(x):
    return jax.nn.gelu(x, approximate=True)

def _silu(x):
    return jax.nn.silu(x)

def _sigmoid(x):
    return jax.nn.sigmoid(x)

def _layernorm(x, axis=-1, eps=1e-05):
    m = jnp.mean(x, axis=axis, keepdims=True)
    v = jnp.var(x, axis=axis, keepdims=True)
    return (x - m) / jnp.sqrt(v + eps)

def _scatter_add(tgt, idx, src, axis=0):
    return tgt.at[idx].add(src)

def _segment_sum(src, seg, n):
    return jax.ops.segment_sum(src, seg, n)
kernel_name = 'mk_seq_postln_d1_jaxref_r4_49c945'

def setup_inputs(seed: int=0):
    np.random.seed(seed)
    _w = jnp.asarray

    def _L0_attn_setup():
        import jax, jax.numpy as jnp
        import numpy as np
        DIM_MODEL = 512
        DQK = 64
        DV = 64
        NUM_HEADS = 32
        NUM_GROUPS = 8
        H_PER_G = NUM_HEADS // NUM_GROUPS
        ROPE_THETA = 10000.0
        RMS_EPS = 1e-06

        def _rope(x):
            d = x.shape[-1]
            s = x.shape[-2]
            inv_freq = 1.0 / ROPE_THETA ** (jnp.arange(0, d, 2, dtype=jnp.float32) / d)
            ang = jnp.arange(s, dtype=jnp.float32)[:, None] * inv_freq[None, :]
            cos, sin = (jnp.cos(ang), jnp.sin(ang))
            x1, x2 = (x[..., :d // 2], x[..., d // 2:])
            return jnp.concatenate([x1 * cos - x2 * sin, x2 * cos + x1 * sin], axis=-1)
        key = jax.random.key(seed)
        k1, k2, k3 = jax.random.split(key, 3)
        b, s = (2, 512)
        concat = NUM_HEADS * DQK + NUM_GROUPS * (DQK + DV)
        x = jax.random.normal(k1, (b, s, DIM_MODEL), dtype=jnp.float32)
        w_in = jax.random.normal(k2, (concat, DIM_MODEL), dtype=jnp.float32) * DIM_MODEL ** (-0.5)
        w_out = jax.random.normal(k3, (DIM_MODEL, NUM_HEADS * DV), dtype=jnp.float32) * (NUM_HEADS * DV) ** (-0.5)
        rms_w = jnp.ones((DIM_MODEL,), dtype=jnp.float32)
        return {'x': x, 'w_in': w_in, 'w_out': w_out, 'rms_w': rms_w}
    _L0_attn_in = _L0_attn_setup()

    def _L0_ffn_setup():
        import jax, jax.numpy as jnp
        import numpy as np

        def ternary_quantize(t, threshold, scale):
            return jnp.where(t > threshold, scale, jnp.where(t < -threshold, -scale, 0.0)).astype(t.dtype)
        key = jax.random.key(seed)
        k1, k2, k3 = jax.random.split(key, 3)
        B, S, D = (4, 1024, 512)
        x = jax.random.normal(k1, (B, S, D), dtype=jnp.float32)
        weight = jax.random.normal(k2, (D, D), dtype=jnp.float32) * 0.02
        rram_variation = jax.random.normal(k3, (D, D), dtype=jnp.float32) * 0.05
        return {'x': x, 'weight': weight, 'rram_variation': rram_variation}
    _L0_ffn_in = _L0_ffn_setup()
    _d = {'L0_attn_x': _L0_attn_in['x'], 'L0_attn_w_in': _L0_attn_in['w_in'], 'L0_attn_w_out': _L0_attn_in['w_out'], 'L0_attn_rms_w': _L0_attn_in['rms_w'], 'L0_ffn_weight': _L0_ffn_in['weight'], 'L0_ffn_rram_variation': _L0_ffn_in['rram_variation']}
    _x0 = _d['L0_attn_x']
    _d['L0_attn_x'] = jax.random.normal(jax.random.fold_in(jax.random.key(seed), 1), (2, 1024, 512), dtype=_x0.dtype)
    del _x0
    return _d

def reference(L0_attn_x, L0_attn_w_in, L0_attn_w_out, L0_attn_rms_w, L0_ffn_weight, L0_ffn_rram_variation):

    def _L0_attn_ref(x, w_in, w_out, rms_w):
        import jax, jax.numpy as jnp
        import numpy as np
        DIM_MODEL = 512
        DQK = 64
        DV = 64
        NUM_HEADS = 32
        NUM_GROUPS = 8
        H_PER_G = NUM_HEADS // NUM_GROUPS
        ROPE_THETA = 10000.0
        RMS_EPS = 1e-06

        def _rope(x):
            d = x.shape[-1]
            s = x.shape[-2]
            inv_freq = 1.0 / ROPE_THETA ** (jnp.arange(0, d, 2, dtype=jnp.float32) / d)
            ang = jnp.arange(s, dtype=jnp.float32)[:, None] * inv_freq[None, :]
            cos, sin = (jnp.cos(ang), jnp.sin(ang))
            x1, x2 = (x[..., :d // 2], x[..., d // 2:])
            return jnp.concatenate([x1 * cos - x2 * sin, x2 * cos + x1 * sin], axis=-1)
        b, s, _ = x.shape
        y = x * jax.lax.rsqrt(jnp.mean(x * x, axis=-1, keepdims=True) + RMS_EPS) * rms_w
        y = jnp.einsum('bsm,cm->bsc', y, w_in)
        cq = NUM_HEADS * DQK
        ck = NUM_GROUPS * DQK
        q, k, v = (y[..., :cq], y[..., cq:cq + ck], y[..., cq + ck:])
        q = q.reshape(b, s, NUM_GROUPS, H_PER_G, DQK).transpose(0, 2, 3, 1, 4)
        k = k.reshape(b, s, NUM_GROUPS, DQK).transpose(0, 2, 1, 3)[:, :, None]
        v = v.reshape(b, s, NUM_GROUPS, DV).transpose(0, 2, 1, 3)[:, :, None]
        q = _rope(q)
        k = _rope(k)
        qk = jnp.einsum('bghsd,bgxpd->bghsp', q, k) * DQK ** (-0.5)
        causal = jnp.tril(jnp.ones((s, s), dtype=bool))
        qk = jnp.where(causal, qk, -jnp.inf)
        attn = jax.nn.softmax(qk, axis=-1)
        o = jnp.einsum('bghsp,bgxpd->bghsd', attn, v)
        o = o.transpose(0, 3, 1, 2, 4).reshape(b, s, NUM_HEADS * DV)
        y = jnp.einsum('bsc,mc->bsm', o, w_out)
        return x + y

    def _L0_ffn_ref(x, weight, rram_variation):
        import jax, jax.numpy as jnp
        import numpy as np

        def ternary_quantize(t, threshold, scale):
            return jnp.where(t > threshold, scale, jnp.where(t < -threshold, -scale, 0.0)).astype(t.dtype)
        TH_X, SC_X = (0.33, 0.5)
        TH_W, SC_W = (0.2, 0.6)
        x_q = ternary_quantize(x, TH_X, SC_X)
        w_q = ternary_quantize(weight, TH_W, SC_W)
        w_rram = w_q + rram_variation
        return jnp.einsum('bsd,od->bso', x_q, w_rram)
    x = L0_attn_x
    x = _layernorm(x + _L0_attn_ref(x, L0_attn_w_in, L0_attn_w_out, L0_attn_rms_w), axis=-1)
    x = _layernorm(x + _L0_ffn_ref(x, L0_ffn_weight, L0_ffn_rram_variation), axis=-1)
    return x

_drawn_inputs = setup_inputs


def setup_inputs(seed=0):
    import zlib

    import numpy as np

    out = dict(_drawn_inputs(seed))
    spreads = {'L0_attn_rms_w': (1.0, 0.2)}
    factors = {}
    for name, (base, spread) in spreads.items():
        noise = np.random.default_rng([zlib.crc32(name.encode()), seed]).standard_normal(out[name].shape)
        drawn = base * np.exp(spread * noise) if base else spread * noise
        out[name] = jnp.asarray(drawn.astype(out[name].dtype))
    for name, factor in factors.items():
        out[name] = (out[name] * factor).astype(out[name].dtype)
    return out
```

```python
from contextlib import ExitStack

import concourse.bass as bass
from concourse import mybir

F32 = mybir.dt.float32
F32R = mybir.dt.float32r
BF16 = mybir.dt.bfloat16
ALU = mybir.AluOpType
ACT = mybir.ActivationFunctionType
AX_X = mybir.AxisListType.X

P = 128
DH = 64
NG = 8
HG = 4
BANK = 512
MASKED = -1e30
ROPE_THETA = 10000.0
RMS_EPS = 1e-6
LN_EPS = 1e-5
TH_X, SC_X = 0.33, 0.5
TH_W, SC_W = 0.2, 0.6

NT = 8
UNITS = NT * (NT + 1) // 2
BODY = 2 * UNITS
CHUNKS = sum(HG * (1 + (s >= 4)) for s in range(NT))
X_KINDS = ("mx", "mr", "qkv", "qt", "kt", "os", "ob", "op", "w", "wo", "fw", "norm")
RING = 4
CARRIED = 2


def first_unit(s):
    return s * (s + 1) // 2


def row_chunks(s):
    return [(0, s + 1)] if s < 4 else [(0, 4), (4, s - 3)]


def chunk_index(s, h, c):
    return sum(HG * len(row_chunks(r)) for r in range(s)) + h * len(row_chunks(s)) + c


class Plan:

    def __init__(self, slots, units):
        self.units = units
        self.ahead = [[] for _ in range(slots)]
        self.behind = [[] for _ in range(slots)]

    def number(self):
        self.x = {}
        for u in range(len(self.ahead)):
            for e in self.ahead[u] + self.behind[u]:
                if e[0] in X_KINDS:
                    self.x[e] = len(self.x)
        self.uses = -(-len(self.x) // RING) * RING
        return self


MAXIMA = ((0, 0, 1), (1, 3, 4), (4, 7, 8), (8, 12, 13), (13, 18, 19), (20, 25, 26), (26, 33, 33), (34, 34, 35), (35, 36, 37), (37, 39, 40), (40, 43, 44), (46, 48, 49), (49, 54, 55), (55, 61, 62), (62, 69, 70), (70, 70, 71))
PROJECT = ((1, 4, 5), (5, 8, 9), (9, 12, 13), (14, 18, 18), (20, 23, 24), (24, 27, 28), (29, 32, 33), (32, 35, 37), (36, 39, 40), (41, 44, 45), (46, 49, 50), (50, 53, 54), (53, 56, 57), (59, 63, 63), (63, 66, 67), (67, 70, 71))
W_OUT = (5, 5)
W_IN = (43, 43, 44, 45)
OUTPUT = ((2, 2, 3, 4, 5), (3, 3, 4, 5, 6), (2, 2, 3, 4, 5), (2, 2, 3, 4, 6), (2, 2, 3, 4, 7), (2, 2, 4, 5, 6), (2, 2, 3, 4, 5), (2, 2, 4, 4, 5), (2, 2, 3, 4, 5), (2, 2, 3, 4, 5), (2, 2, 3, 4, 5), (2, 2, 3, 4, 5), (2, 2, 3, 4, 5), (2, 2, 4, 4, 5), (2, 2, 3, 4, 5), (2, 1, 3, 5, 6), (2, 2, 3, 4, 5))


def body_plan(opening, last):
    plan = Plan(BODY + (7 if last else 0), BODY)
    for b, s in [(0, s) for s in range(2, NT)] + [(1, s) for s in range(NT)] + [(2, 0), (2, 1)]:
        if last and b == 2:
            continue
        chunks = [(h, c) for h in range(HG) for c in range(len(row_chunks(s)))]
        lo, hi, row = MAXIMA[b * NT + s - 2]
        for n, (h, c) in enumerate(chunks):
            plan.ahead[lo + (hi - lo + 1) * n // len(chunks)].append(("mx", b, s, h, c))
        plan.ahead[row].append(("mr", b, s))
    for n, (u, qt, kt) in enumerate(PROJECT):
        b, t = divmod(n + NT - CARRIED, NT)
        if not last or b < 2:
            plan.behind[u].append(("qkv", b, t))
            plan.behind[qt].append(("qt", b, t))
            plan.behind[kt].append(("kt", b, t))
    for c, u in enumerate(W_OUT):
        plan.behind[u].append(("wo", c))
    if not last:
        for c, u in enumerate(W_IN):
            plan.behind[u].append(("w", c))
    else:
        for n in range(4):
            plan.behind[46 + 4 * n].append(("fw", n))
    for b, s in [(-1, NT - 1)] + [(b, s) for b in range(2) for s in range(NT)]:
        end = b * UNITS + first_unit(s + 1) - 1
        if (b, s) == (-1, NT - 1) and opening or (b, s) == (1, NT - 1) and not last:
            continue
        for kind, lag in zip(("oe", "os", "ob", "oh", "op"), OUTPUT[b * NT + s + 1]):
            plan.behind[end + lag].append((kind, b, s))
    return plan.number()


def first_plan():
    norm = [("sq", 0), ("xn", 0), ("xn", 1)]
    for t in range(2 * NT):
        if t + 2 < 2 * NT:
            if (t + 2) % 4 == 0:
                norm.append(("sq", (t + 2) // 4))
            norm.append(("xn", t + 2))
        norm.append(("norm", t))
    rest = [("consts",)] + [("w", c) for c in range(4)]
    for t in range(NT - CARRIED + 1):
        if t < NT - CARRIED:
            rest.append(("qkv", 2, t))
        if t:
            rest += [("qt", 2, t - 1), ("kt", 2, t - 1)]
        if t in (2, 4):
            rest += [("mx", 2, t // 2 - 1, h, 0) for h in range(HG)]
        if t in (3, 5):
            rest.append(("mr", 2, (t - 3) // 2))
    start = norm.index(("norm", 3)) + 1
    order = norm[:start]
    norm = norm[start:]
    done = 0
    for n, e in enumerate(rest):
        order.append(e)
        upto = len(norm) * (n + 1) // len(rest)
        order += norm[done:upto]
        done = upto
    plan = Plan(1, 0)
    plan.ahead[0] = order
    return plan.number()


def seq_block(nc, x, w_in, w_out, rms_w, ffn_w, ffn_r, cos, sin, ident_d, tri_d, trit_d, out):
    B, S, D = x.shape
    TT = B * S // P
    KC = D // P
    QC = HG * DH
    WC = QC + 2 * DH
    NQ = NG * QC
    assert B == 2 and S == NT * P and D == BANK and WC <= BANK
    LAST = NG - 1

    first, opening = first_plan(), body_plan(True, False)
    body, final = body_plan(False, False), body_plan(False, True)
    first.base = 0, 0
    opening.base = first.uses, len(first.x)
    body.base = final.base = (opening.base[0] + opening.uses - body.uses, opening.base[1] + len(opening.x) - len(body.x))
    opening.past, body.past, final.past = first, body, body
    assert list(body.x)[-2 * RING:] == list(opening.x)[-2 * RING:]

    x_v = x.rearrange("b (t p) d -> p (b t) d", p=P)
    out_v = out.rearrange("b (t p) d -> p (b t) d", p=P)

    with ExitStack() as ctx:
        def sb(name, shape, dt=F32):
            return ctx.enter_context(nc.sbuf_tensor(name, shape, dt))

        def ps(name):
            return ctx.enter_context(nc.psum_tensor(name, [P, BANK], F32))

        def sem(name):
            return ctx.enter_context(nc.semaphore(name))

        acc = sb("acc", [P, TT, D])
        yt_hi = sb("yt_hi", [P, KC, TT * P], F32R)
        yt_lo = sb("yt_lo", [P, KC, TT * P], F32R)
        ffn_hi = yt_hi[:, :, 0:D]
        ffn_lo = yt_lo[:, :, 0:D]
        cos_sb = sb("cos_sb", [P, NT, DH])
        sin_sb = sb("sin_sb", [P, NT, DH])
        ident = sb("ident", [P, P])
        ident_r = sb("ident_r", [P, P], F32R)
        trit_r = sb("trit_r", [P, P], F32R)
        mask = sb("mask", [P, BANK])
        ones = sb("ones", [P, 1])
        rms = sb("rms", [P, KC])
        ss = sb("ss", [P, TT])
        rstd = sb("rstd", [P, TT])
        neg_half = sb("neg_half", [P, TT])
        raw = sb("raw", [P, 3, D])
        wout_raw = raw[:, 0:2, :].rearrange("p a (b c) -> p (a b) c", b=2)
        win_hi = sb("win_hi", [P, KC, WC], F32R)
        win_lo = sb("win_lo", [P, KC, WC], F32R)
        wout_hi = sb("wout_hi", [P, 2, D], F32R)
        wout_lo = sb("wout_lo", [P, 2, D], F32R)
        rope_a = sb("rope_a", [P, HG + 1, DH])
        rope_b = sb("rope_b", [P, HG + 1, DH])
        roped = sb("roped", [P, HG + 1, DH])
        stack = sb("stack", [P, HG + 2, P], F32R)
        q_t = sb("q_t", [P, HG, S], F32R)
        k_t = sb("k_t", [P, 2, 2, S], F32R)
        v_sb = sb("v_sb", [P, 2, NT, P], F32R)
        q_shift = sb("q_shift", [P, 2, HG, P], F32R)
        neg_max = sb("neg_max", [P, HG])
        row_max = sb("row_max", [P, HG])
        neg_max_r = sb("neg_max_r", [P, HG], F32R)
        junk = sb("junk", [P, 2, BANK], BF16)
        prob = sb("prob", [P, 3, BANK])
        prob_hi = sb("prob_hi", [P, 2, BANK], F32R)
        prob_lo = sb("prob_lo", [P, 2, BANK], F32R)
        prob_sum = sb("prob_sum", [P, 2, BANK])
        o_low = sb("o_low", [DH, BANK])
        o_raw = sb("o_raw", [P, 2, P])
        recip = sb("recip", [P, HG])
        o_t = sb("o_t", [P, 2, P])
        o_hi = sb("o_hi", [P, 2, P], F32R)
        o_lo = sb("o_lo", [P, 2, P], F32R)
        xq_t = q_t[:, 0:2, 0:D].rearrange("p e (k q) -> p e k q", k=KC)
        stats = sb("stats", [P, 2, 2, 6])
        moments = sb("moments", [P, 2, 2, 2])
        inv_std = sb("inv_std", [P, 2, 2])
        shift = sb("shift", [P, 2])

        st_ps = [ps("st0"), ps("st1")]
        ot_ps = [ps("ot0"), ps("ot1")]
        x_ps = [ps(f"x{n}") for n in range(RING)]

        waited = sem("waited")
        ident_in = sem("ident_in")
        rms_in = sem("rms_in")
        consts_in = sem("consts_in")
        x_in = [sem(f"x_in{n}") for n in range(4)]
        ffn_in = [sem(f"ffn_in{n}") for n in range(2)]
        win_in = sem("win_in")
        wout_in = sem("wout_in")
        consts_set = sem("consts_set")
        consts_cast = sem("consts_cast")
        ss_done = sem("ss_done")
        rstd_mid = sem("rstd_mid")
        rstd_done = sem("rstd_done")
        xn_done = sem("xn_done")
        y_hi_done = sem("y_hi_done")
        y_lo_done = sem("y_lo_done")
        tern_step = sem("tern_step")
        ffn_w_done = sem("ffn_w_done")
        ffn_hi_done = sem("ffn_hi_done")
        ffn_lo_done = sem("ffn_lo_done")
        doubled = sem("doubled")

        x_full = sem("x_full")
        win_hi_done = sem("win_hi_done")
        win_done = sem("win_done")
        wout_hi_done = sem("wout_hi_done")
        wout_done = sem("wout_done")
        roped_ab = sem("roped_ab")
        rope_sum = sem("rope_sum")
        stack_hi = sem("stack_hi")
        stack_done = sem("stack_done")
        v_hi_done = sem("v_hi_done")
        v_done = sem("v_done")
        qt_done = sem("qt_done")
        kt_done = sem("kt_done")
        q_shift_in = [sem(f"q_shift_in{n}") for n in range(2)]
        mx_done = sem("mx_done")
        neg_max_done = sem("neg_max_done")
        shift_done = sem("shift_done")
        st_done = sem("st_done")
        prob_done = sem("prob_done")
        prob_hi_done = sem("prob_hi_done")
        prob_lo_done = sem("prob_lo_done")
        sum_done = sem("sum_done")
        pv_done = sem("pv_done")
        o_low_done = sem("o_low_done")
        o_raw_done = sem("o_raw_done")
        recip_done = sem("recip_done")
        o_t_done = sem("o_t_done")
        o_hi_done = sem("o_hi_done")
        o_lo_done = sem("o_lo_done")
        acc_done = sem("acc_done")

        stat_done = [sem(f"stat_done{n}") for n in (1, 2)]
        var_done = [sem(f"var_done{n}") for n in (1, 2)]
        inv_step = [sem(f"inv_step{n}") for n in (1, 2)]
        inv_done = [sem(f"inv_done{n}") for n in (1, 2)]
        x1_done = sem("x1_done")
        below_done = sem("below_done")
        tern_done = sem("tern_done")
        tern_t_full = sem("tern_t_full")
        xq_done = sem("xq_done")
        ffn_done = sem("ffn_done")
        x2_done = sem("x2_done")
        out_done = sem("out_done")
        stored = sem("stored")

        block = ctx.enter_context(nc.Block())

        def wait(eng, s, g, per_body, count):
            if isinstance(g, int):
                if g * per_body + count > 0:
                    eng.wait_ge(s, g * per_body + count)
            else:
                assert per_body + count > 0
                eng.wait_ge(s, g * per_body + count)

        def met(eng):
            eng.sem_inc(waited, 1)

        def x_bank(plan, e):
            return x_ps[(plan.base[0] + plan.x[e]) % RING]

        def wait_x_full(eng, plan, g, e):
            wait(eng, x_full, max(g, 0) if plan is first or plan is opening else g, len(body.x), plan.base[1] + plan.x[e] + 1)
            return x_bank(plan, e)

        def wait_x_free(eng, plan, g, e):
            n, past, back = plan.x[e] - RING, plan, 0
            if n < 0:
                if plan is first:
                    return
                past, back = plan.past, 2
                n += past.uses
                while n >= len(past.x):
                    n -= RING
            kind, *what = list(past.x)[n]
            tile = (what[0] - back) * NT + what[1] + 1 if len(what) >= 2 else 0
            assert len(what) >= 2 or not back or kind == "norm"
            if kind == "mx":
                wait(eng, mx_done, g, 2 * CHUNKS, (what[0] - back) * CHUNKS + chunk_index(*what[1:]) + 1)
            elif kind == "mr":
                wait(eng, shift_done, g, 2 * NT, tile)
            elif kind == "qkv":
                wait(eng, v_done, g, 2 * NT, tile)
            elif kind == "qt":
                wait(eng, qt_done, g, 2 * NT, tile)
            elif kind == "kt":
                wait(eng, kt_done, g, 2 * NT, tile)
            elif kind == "os":
                wait(eng, recip_done, g, 2 * NT, tile)
            elif kind == "ob":
                wait(eng, o_t_done, g, 2 * NT, tile)
            elif kind == "op":
                wait(eng, acc_done, g, 2 * NT, tile)
            elif kind == "norm":
                eng.wait_ge(y_lo_done, what[0] + 1)
            elif kind == "w":
                wait(eng, win_done, g, 4, 4 + what[0] + 1)
            elif kind == "wo":
                wait(eng, wout_done, g, 2, what[0] + 1)
            elif kind == "fw":
                eng.wait_ge(ffn_lo_done, what[0] + 1)

        def unit_of(u):
            b, u = divmod(u, UNITS)
            s = max(s for s in range(NT) if first_unit(s) <= u)
            return b, s, u - first_unit(s)

        def over_bodies(eng, one):
            one(-1, first)
            one(0, opening)
            with eng.Fori(1, LAST) as g:
                one(g, body)
            one(LAST, final)

        NORM, TERN, FFN, OUT = range(4)

        def over_tiles(eng, step):
            for k in range(4):
                step(k, k)
            with eng.Fori(1, TT // 4) as m:
                for e in range(4):
                    step(m * 4 + e, e)
            for k in range(TT, TT + OUT):
                step(k, k % 4)

        def runs(k, lag):
            return not isinstance(k, int) or 0 <= k - lag < TT

        def wait_tiles(eng, s, count):
            if not isinstance(count, int) or count > 0:
                eng.wait_ge(s, count)

        def acc_tile(t):
            return acc[:, bass.ds(t, 1), :].rearrange("p a d -> p (a d)")

        def q_tile(t):
            return q_t[:, :, t * P:(t + 1) * P]

        @block.sync
        def _(sp):
            def load_x(n):
                sp.dma_start(acc[:, 4 * n:4 * n + 4, :], x_v[:, 4 * n:4 * n + 4, :]).then_inc(x_in[n], 16)

            def load_win(g):
                sp.dma_start(raw[:, 0:2, :], w_in[bass.ds(g * QC, QC), :].rearrange("(a p) d -> p a d", p=P)
                             ).then_inc(win_in, 16)
                sp.dma_start(raw[0:DH, 2, :], w_in[bass.ds(g * DH + NQ, DH), :]).then_inc(win_in, 16)
                sp.dma_start(raw[DH:P, 2, :], w_in[bass.ds(g * DH + (NQ + NG * DH), DH), :]
                             ).then_inc(win_in, 16)

            def load_wout(g):
                sp.dma_start(wout_raw[:, :, :], w_out[:, bass.ds(g * QC, QC)].rearrange("(a p) c -> p a c", p=P)
                             ).then_inc(wout_in, 16)

            load_x(0)
            sp.dma_start(ident[:, :], ident_d).then_inc(ident_in, 16)
            load_win(0)
            sp.dma_start(rms[:, :], rms_w).then_inc(rms_in, 16)
            sp.dma_start(mask[:, BANK - P:BANK], tri_d).then_inc(consts_in, 16)
            sp.dma_start(prob_sum[:, 0, 0:P], trit_d).then_inc(consts_in, 16)
            sp.dma_start(cos_sb[:, :, :], cos.rearrange("(t p) d -> p t d", p=P)).then_inc(consts_in, 16)
            sp.dma_start(sin_sb[:, :, :], sin.rearrange("(t p) d -> p t d", p=P)).then_inc(consts_in, 16)
            for n in range(1, 4):
                load_x(n)

            def one(g, plan):
                for u in range(len(plan.ahead)):
                    for e in plan.ahead[u] + plan.behind[u]:
                        if e[0] == "mr":
                            _, b, s = e
                            wait(sp, qt_done, g, 2 * NT, b * NT + s + 1)
                            met(sp)
                            k = (b * NT + s) % 2
                            b0, s0 = divmod(b * NT + s - 2, NT)
                            wait(sp, st_done, g, BODY, b0 * UNITS + first_unit(s0 + 1))
                            sp.dma_start(q_shift[0:DH, k, :, :].bitcast(F32), q_tile(s)[0:DH, :, :].bitcast(F32)).then_inc(q_shift_in[k], 16)
                        elif e == ("wo", 1) and plan is not final:
                            wait(sp, wout_done, g, 2, 2)
                            met(sp)
                            load_win(g + 1)
                        elif e == ("w", 3):
                            wait(sp, win_done, g, 4, 8)
                            met(sp)
                            load_wout(g + 1)
                        elif e[0] == "fw":
                            n = e[1]
                            sp.wait_ge(wout_done, 2 * NG)
                            if n:
                                sp.wait_ge(ffn_lo_done, n)
                            sp.dma_start(raw[:, 0, :], ffn_w[n * P:(n + 1) * P, :]).then_inc(ffn_in[0], 16)
                            sp.dma_start(raw[:, 1, :], ffn_r[n * P:(n + 1) * P, :]).then_inc(ffn_in[1], 16)

            over_bodies(sp, one)

            def step(k, e):
                if runs(k, OUT):
                    sp.wait_ge(out_done, k - OUT + 1)
                    met(sp)
                    sp.dma_start(out_v[:, bass.ds(k - OUT, 1), :], acc[:, bass.ds(k - OUT, 1), :]).then_inc(stored, 16)

            over_tiles(sp, step)
            sp.wait_ge(stored, 16 * TT)

        @block.gpsimd
        def _(pool):
            pool.memset(neg_half[:, :], -0.5).then_inc(consts_set, 1)
            pool.memset(ones[:, :], 1.0).then_inc(consts_set, 1)
            pool.memset(mask[:, 0:BANK - P], 0.0).then_inc(consts_set, 1)
            pool.memset(stack[:, HG + 1, :].bitcast(F32), 0.0).then_inc(consts_set, 1)
            pool.wait_ge(consts_set, 4)
            pool.memset(stack[:, HG + 1, DH:DH + 1].bitcast(F32), 1.0).then_inc(consts_set, 1)
            def one(g, plan):
                for u in range(len(plan.ahead)):
                    if u < plan.units:
                        b, s, j = unit_of(u)
                        k = b * NT + s
                        total = prob_sum[:, k % 2, :]
                        if s == 0:
                            wait(pool, recip_done, g, 2 * NT, k - 1)
                            wait(pool, prob_done, g, BODY, u + 1)
                            met(pool)
                            pool.tensor_scalar(total, prob[:, u % 3, :], 1.0, None, ALU.mult).then_inc(sum_done, 1)
                        elif j:
                            if j == 1:
                                wait(pool, recip_done, g, 2 * NT, k - 1)
                            else:
                                wait(pool, sum_done, g, BODY, u)
                            wait(pool, prob_done, g, BODY, u + 1)
                            pool.tensor_tensor(total, prob[:, (u - 1) % 3, :] if j == 1 else total,
                                               prob[:, u % 3, :], ALU.add).then_inc(sum_done, 2 if j == 1 else 1)
                    for e in plan.ahead[u] + plan.behind[u]:
                        if e[0] == "sq":
                            n = e[1]
                            some = slice(4 * n, 4 * n + 4)
                            pool.wait_ge(ss_done, 4 * n + 4)
                            pool.tensor_scalar(rstd[:, some], ss[:, some], 1.0 / D, RMS_EPS, ALU.mult, ALU.add
                                               ).then_inc(rstd_mid, 1)
                            pool.wait_ge(rstd_mid, n + 1)
                            pool.tensor_tensor(rstd[:, some], rstd[:, some], neg_half[:, some], ALU.pow
                                               ).then_inc(rstd_done, 1)
                        elif e[0] == "qkv":
                            _, b, t = e
                            n = b * NT + t
                            wait(pool, roped_ab, g, 2 * NT, n + 1)
                            wait(pool, kt_done, g, 2 * NT, n)
                            pool.tensor_tensor(roped[:, :, :], rope_a[:, :, :], rope_b[:, :, :], ALU.add
                                               ).then_inc(rope_sum, 1)
                            wait(pool, rope_sum, g, 2 * NT, n + 1)
                            met(pool)
                            pool.tensor_scalar(stack[:, 0:HG, 0:DH], roped[:, 0:HG, :], 1.0, None, ALU.mult
                                               ).then_inc(stack_hi, 1)
                            pool.tensor_scalar(stack[:, HG, :].rearrange("p (a d) -> p a d", a=2),
                                               roped[:, HG:HG + 1, :].to_broadcast([P, 2, DH]),
                                               1.0, None, ALU.mult).then_inc(stack_hi, 1)
                            wait(pool, stack_hi, g, 4 * NT, 2 * n + 2)
                            pool.tensor_tensor(stack[:, 0:HG, DH:P], roped[:, 0:HG, :],
                                               stack[:, 0:HG, 0:DH].bitcast(F32), ALU.subtract).then_inc(stack_done, 1)
                            pool.tensor_tensor(stack[:, HG + 1, 0:DH], roped[:, HG, :],
                                               stack[:, HG, 0:DH].bitcast(F32), ALU.subtract).then_inc(stack_done, 1)

            over_bodies(pool, one)

            def inverse_std(n, tile, e):
                inv = inv_std[:, n, e % 2:e % 2 + 1]
                wait_tiles(pool, var_done[n], tile + 1)
                if n == 1:
                    wait_tiles(pool, out_done, tile - 1)
                met(pool)
                pool.tensor_scalar(inv, moments[:, n, e % 2, 1:2], 1.0, LN_EPS, ALU.mult, ALU.add
                                   ).then_inc(inv_step[n], 1)
                wait_tiles(pool, inv_step[n], tile + 1)
                pool.tensor_tensor(inv, inv, neg_half[:, 0:1], ALU.pow).then_inc(inv_done[n], 1)
                if n == 1:
                    wait_tiles(pool, inv_done[n], tile * 2 + 1)
                    met(pool)
                    pool.tensor_scalar(shift[:, e % 2:e % 2 + 1], moments[:, n, e % 2, 0:1], inv, -1.0,
                                       ALU.mult, ALU.mult).then_inc(inv_done[n], 1)

            def step(k, e):
                if runs(k, NORM):
                    inverse_std(0, k - NORM, e - NORM)
                if runs(k, OUT):
                    inverse_std(1, k - OUT, e - OUT)

            over_tiles(pool, step)

        @block.scalar
        def _(act):
            def one(g, plan):
                for u in range(len(plan.ahead)):
                    if u < plan.units:
                        wait(act, st_done, g, BODY, u + 1)
                        wait(act, prob_hi_done, g, BODY, u - 2)
                        wait(act, prob_lo_done, g, BODY, u - 2)
                        wait(act, sum_done, g, BODY, u - 2)
                        act.activation(prob[:, u % 3, :], st_ps[u % 2][:, :], ACT.Exp, scale=DH ** -0.5
                                       ).then_inc(prob_done, 1)
                        wait(act, prob_done, g, BODY, u + 1)
                        wait(act, pv_done, g, BODY, u - 1)
                        act.activation(prob_hi[:, u % 2, :], prob[:, u % 3, :], ACT.Copy).then_inc(prob_hi_done, 1)
                    for e in plan.ahead[u] + plan.behind[u]:
                        if e[0] == "sq":
                            act.wait_ge(x_in[e[1]], 16)
                            for t in range(4 * e[1], 4 * e[1] + 4):
                                if t:
                                    act.wait_ge(ss_done, t)
                                act.activation(junk[:, 0, :], acc[:, t, :], ACT.Square, accum_out=ss[:, t:t + 1]
                                               ).then_inc(ss_done, 1)
                        elif e[0] == "norm":
                            t = e[1]
                            bank = wait_x_full(act, plan, g, e)
                            act.activation(yt_hi[:, :, t * P:(t + 1) * P],
                                           bank[:, :].rearrange("p (k q) -> p k q", k=KC), ACT.Copy
                                           ).then_inc(y_hi_done, 1)
                        elif e[0] == "mr":
                            _, b, s = e
                            bank = wait_x_full(act, plan, g, e)
                            b0, s0 = divmod(b * NT + s - 2, NT)
                            wait(act, st_done, g, BODY, b0 * UNITS + first_unit(s0 + 1))
                            act.activation(q_shift[DH:DH + 1, (b * NT + s) % 2, :, :],
                                           bank[0:1, :].rearrange("p (h q) -> p h q", h=HG), ACT.Copy
                                           ).then_inc(shift_done, 1)
                        elif e[0] == "w":
                            bank = wait_x_full(act, plan, g, e)
                            if plan is first:
                                act.wait_ge(rms_in, 16)
                            act.activation(win_hi[:, e[1], :], bank[:, 0:WC], ACT.Copy, scale=rms[:, e[1]:e[1] + 1]
                                           ).then_inc(win_hi_done, 1)
                        elif e[0] == "wo":
                            bank = wait_x_full(act, plan, g, e)
                            act.activation(wout_hi[:, e[1], :], bank[:, :], ACT.Copy).then_inc(wout_hi_done, 1)
                        elif e[0] == "fw":
                            bank = wait_x_full(act, plan, g, e)
                            act.activation(ffn_hi[:, :, e[1] * P:(e[1] + 1) * P],
                                           bank[:, :].rearrange("p (k q) -> p k q", k=KC), ACT.Copy
                                           ).then_inc(ffn_hi_done, 1)
                        elif e[0] == "qt":
                            _, b, t = e
                            bank = wait_x_full(act, plan, g, e)
                            wait(act, st_done, g, BODY, (b - 1) * UNITS + first_unit(t + 1))
                            act.activation(q_tile(t), bank[:, :].rearrange("p (h q) -> p h q", h=HG), ACT.Copy
                                           ).then_inc(qt_done, 1)
                        elif e[0] == "kt":
                            _, b, t = e
                            bank = wait_x_full(act, plan, g, e)
                            wait(act, st_done, g, BODY, (b - 1) * UNITS)
                            act.activation(k_t[:, b % 2, :, t * P:(t + 1) * P],
                                           bank[:, 0:2 * P].rearrange("p (a q) -> p a q", a=2), ACT.Copy
                                           ).then_inc(kt_done, 1)
                        elif e[0] == "oe":
                            _, b, s = e
                            k = b * NT + s
                            wait(act, pv_done, g, BODY, b * UNITS + first_unit(s + 1))
                            wait(act, o_raw_done, g, 2 * NT, k)
                            act.activation(o_low[:, :], ot_ps[k % 2][DH:P, :], ACT.Copy).then_inc(o_low_done, 1)
                        elif e[0] == "oh":
                            _, b, s = e
                            kk = b * NT + s
                            wait(act, o_t_done, g, 2 * NT, kk + 1)
                            wait(act, acc_done, g, 2 * NT, kk)
                            act.activation(o_hi[:, :, :], o_t[:, :, :], ACT.Copy).then_inc(o_hi_done, 1)

            over_bodies(act, one)

            def step(k, e):
                if runs(k, TERN):
                    t, n = k - TERN, (e - TERN) % 2
                    wait_tiles(act, tern_t_full, t + 1)
                    wait_tiles(act, ffn_done, t - 1)
                    act.activation(xq_t[:, n, :, :], x_ps[n][:, :].rearrange("p (k q) -> p k q", k=KC), ACT.Copy
                                   ).then_inc(xq_done, 1)
                if runs(k, OUT):
                    t, n = k - OUT, (e - OUT) % 2
                    wait_tiles(act, inv_done[1], t * 2 + 2)
                    act.activation(acc_tile(t), acc_tile(t), ACT.Identity, bias=shift[:, n:n + 1],
                                   scale=inv_std[:, 1, n:n + 1]).then_inc(out_done, 1)

            over_tiles(act, step)

        @block.vector
        def _(dve):
            def one(g, plan):
                def events(some):
                    for e in some:
                        if e[0] == "consts":
                            dve.wait_ge(consts_in, 16 * 4)
                            dve.wait_ge(consts_set, 5)
                            dve.tensor_copy(ident_r[:, :], ident[:, :]).then_inc(consts_cast, 1)
                            dve.tensor_copy(trit_r[:, :], prob_sum[:, 0, 0:P]).then_inc(consts_cast, 1)
                            dve.wait_ge(rms_in, 16)
                        elif e[0] == "xn":
                            t = e[1]
                            dve.wait_ge(rstd_done, t // 4 + 1)
                            dve.tensor_scalar(prob[:, t % 3, :], acc[:, t, :], rstd[:, t:t + 1], None, ALU.mult
                                              ).then_inc(xn_done, 1)
                        elif e[0] == "norm":
                            t = e[1]
                            dve.wait_ge(y_hi_done, t + 1)
                            dve.tensor_tensor(yt_lo[:, :, t * P:(t + 1) * P],
                                              x_bank(plan, e)[:, :].rearrange("p (k q) -> p k q", k=KC),
                                              yt_hi[:, :, t * P:(t + 1) * P].bitcast(F32), ALU.subtract
                                              ).then_inc(y_lo_done, 1)
                        elif e[0] == "mx":
                            _, b, s, h, c = e
                            n = b * CHUNKS + chunk_index(s, h, c)
                            bank = wait_x_full(dve, plan, g, e)
                            wait(dve, neg_max_done, g, 2 * NT, b * NT + s)
                            cols = row_chunks(s)[c][1] * P
                            if s >= 4 and c == 0:
                                dve.reduce_max(row_max[:, h:h + 1], bank[:, :], AX_X).then_inc(mx_done, 1)
                            else:
                                wait(dve, mx_done, g, 2 * CHUNKS, n - 1)
                                met(dve)
                                dve.tensor_tensor_reduce(out=junk[:, n % 2, 0:cols], in0=bank[:, 0:cols],
                                                         in1=mask[:, BANK - cols:BANK], scale=-1.0, scalar=3e38,
                                                         op0=ALU.add, op1=ALU.min,
                                                         accum_out=neg_max[:, h:h + 1]).then_inc(mx_done, 1)
                        elif e[0] == "mr":
                            _, b, s = e
                            wait(dve, mx_done, g, 2 * CHUNKS, b * CHUNKS + chunk_index(s, HG, 0))
                            wait(dve, shift_done, g, 2 * NT, b * NT + s)
                            if s >= 4:
                                dve.scalar_tensor_tensor(out=neg_max_r[:, :], in0=row_max[:, :], scalar=-1.0,
                                                         in1=neg_max[:, :], op0=ALU.mult, op1=ALU.min
                                                         ).then_inc(neg_max_done, 1)
                            else:
                                dve.tensor_copy(neg_max_r[:, :], neg_max[:, :]).then_inc(neg_max_done, 1)
                        elif e[0] == "w":
                            k, bank = e[1], x_bank(plan, e)
                            wait(dve, win_hi_done, g, 4, 4 + k + 1)
                            dve.scalar_tensor_tensor(out=win_lo[:, k, :], in0=bank[:, 0:WC], scalar=rms[:, k:k + 1],
                                                     in1=win_hi[:, k, :].bitcast(F32), op0=ALU.mult, op1=ALU.subtract
                                                     ).then_inc(win_done, 1)
                        elif e[0] == "wo":
                            k, bank = e[1], x_bank(plan, e)
                            wait(dve, wout_hi_done, g, 2, k + 1)
                            dve.tensor_tensor(wout_lo[:, k, :], bank[:, :], wout_hi[:, k, :].bitcast(F32),
                                              ALU.subtract).then_inc(wout_done, 1)
                        elif e[0] == "fw":
                            n, bank = e[1], x_bank(plan, e)
                            dve.wait_ge(ffn_in[0], 16 * (n + 1))
                            dve.wait_ge(ffn_in[1], 16 * (n + 1))
                            dve.tensor_scalar(raw[:, 2, :], raw[:, 0, :], TH_W, SC_W, ALU.is_gt, ALU.mult
                                              ).then_inc(tern_step, 1)
                            dve.tensor_scalar(raw[:, 0, :], raw[:, 0, :], -TH_W, SC_W, ALU.is_lt, ALU.mult
                                              ).then_inc(tern_step, 1)
                            dve.wait_ge(tern_step, 3 * n + 2)
                            dve.tensor_tensor(raw[:, 2, :], raw[:, 2, :], raw[:, 0, :], ALU.subtract
                                              ).then_inc(tern_step, 1)
                            dve.wait_ge(tern_step, 3 * n + 3)
                            dve.tensor_tensor(raw[:, 2, :], raw[:, 2, :], raw[:, 1, :], ALU.add).then_inc(ffn_w_done, 1)
                            dve.wait_ge(ffn_hi_done, n + 1)
                            dve.tensor_tensor(ffn_lo[:, :, n * P:(n + 1) * P],
                                              bank[:, :].rearrange("p (k q) -> p k q", k=KC),
                                              ffn_hi[:, :, n * P:(n + 1) * P].bitcast(F32), ALU.subtract
                                              ).then_inc(ffn_lo_done, 1)
                        elif e[0] == "qkv":
                            _, b, t = e
                            n = b * NT + t
                            bank = wait_x_full(dve, plan, g, e)
                            heads = bank[:, 0:QC + DH].rearrange("p (h d) -> p h d", d=DH)
                            wait(dve, rope_sum, g, 2 * NT, n)
                            dve.tensor_tensor(rope_a[:, :, :], heads,
                                              cos_sb[:, t:t + 1, :].to_broadcast([P, HG + 1, DH]), ALU.mult)
                            dve.tensor_tensor(
                                rope_b[:, :, :].rearrange("p h (a d) -> p h a d", a=2),
                                heads.rearrange("p h (a d) -> p h a d", a=2)[:, :, ::-1, :],
                                sin_sb[:, t:t + 1, :].to_broadcast([P, HG + 1, DH])
                                .rearrange("p h (a d) -> p h a d", a=2), ALU.mult).then_inc(roped_ab, 1)
                            wait(dve, pv_done, g, BODY, (b - 1) * UNITS)
                            dve.tensor_copy(v_sb[:, b % 2, t, 0:DH], bank[:, QC + DH:WC]).then_inc(v_hi_done, 1)
                            wait(dve, v_hi_done, g, 2 * NT, n + 1)
                            dve.tensor_tensor(v_sb[:, b % 2, t, DH:P], bank[:, QC + DH:WC],
                                              v_sb[:, b % 2, t, 0:DH].bitcast(F32), ALU.subtract).then_inc(v_done, 1)
                        elif e[0] == "oe":
                            _, b, s = e
                            kk = b * NT + s
                            wait(dve, o_low_done, g, 2 * NT, kk + 1)
                            wait(dve, o_t_done, g, 2 * NT, kk)
                            top = ot_ps[kk % 2][0:DH, :].rearrange("p (c a q) -> p a c q", c=2, a=2)
                            low = o_low[:, :].rearrange("p (c a q) -> p a c q", c=2, a=2)
                            dve.tensor_tensor(o_raw[0:DH, :, :], top[:, 0], low[:, 0], ALU.add)
                            dve.tensor_tensor(o_raw[DH:P, :, :], top[:, 1], low[:, 1], ALU.add).then_inc(o_raw_done, 1)
                        elif e[0] == "os":
                            _, b, s = e
                            bank = wait_x_full(dve, plan, g, e)
                            wait(dve, o_t_done, g, 2 * NT, b * NT + s)
                            dve.reciprocal(recip[:, :], bank[:, 0:HG]).then_inc(recip_done, 1)
                        elif e[0] == "ob":
                            _, b, s = e
                            kk = b * NT + s
                            bank = wait_x_full(dve, plan, g, e)
                            wait(dve, o_raw_done, g, 2 * NT, kk + 1)
                            wait(dve, o_lo_done, g, 2 * NT, kk)
                            dve.tensor_tensor(o_t[:, :, :], bank[:, 0:2 * P].rearrange("p (c q) -> p c q", c=2),
                                              o_raw[:, :, :], ALU.mult).then_inc(o_t_done, 1)
                        elif e[0] == "oh":
                            _, b, s = e
                            kk = b * NT + s
                            wait(dve, o_hi_done, g, 2 * NT, kk + 1)
                            dve.tensor_tensor(o_lo[:, :, :], o_t[:, :, :], o_hi[:, :, :].bitcast(F32), ALU.subtract
                                              ).then_inc(o_lo_done, 1)
                        elif e[0] == "op":
                            _, b, s = e
                            bank = wait_x_full(dve, plan, g, e)
                            tile = acc[:, (b * NT + s) % TT, :]
                            wait(dve, acc_done, g, 2 * NT, (b - 1) * NT + s)
                            if plan is opening:
                                dve.scalar_tensor_tensor(out=tile, in0=tile, scalar=2.0, in1=bank[:, :], op0=ALU.mult,
                                                         op1=ALU.add).then_inc(acc_done, 1)
                            else:
                                dve.tensor_tensor(tile, tile, bank[:, :], ALU.add).then_inc(acc_done, 1)

                if plan is opening:
                    dve.tensor_scalar(acc[:, TT - 1, :], acc[:, TT - 1, :], 2.0, None, ALU.mult).then_inc(doubled, 1)
                    dve.wait_ge(doubled, 1)
                for u in range(len(plan.ahead)):
                    events(plan.ahead[u])
                    if u < plan.units:
                        wait(dve, prob_hi_done, g, BODY, u + 1)
                        wait(dve, pv_done, g, BODY, u - 1)
                        dve.tensor_tensor(prob_lo[:, u % 2, :], prob[:, u % 3, :], prob_hi[:, u % 2, :].bitcast(F32),
                                          ALU.subtract).then_inc(prob_lo_done, 1)
                    events(plan.behind[u])

            over_bodies(dve, one)

            def moments_of(n, tile, e, data):
                wait_tiles(dve, inv_done[n], (tile - 1) * (n + 1))
                met(dve)
                dve.bn_stats(stats[:, n, e % 2, :], data).then_inc(stat_done[n], 1)
                wait_tiles(dve, stat_done[n], tile + 1)
                met(dve)
                dve.bn_aggr(moments[:, n, e % 2, :], stats[:, n, e % 2, :]).then_inc(var_done[n], 1)

            def step(k, e):
                if runs(k, NORM):
                    moments_of(0, k - NORM, e - NORM, acc_tile(k - NORM))
                if runs(k, TERN):
                    t, n = k - TERN, (e - TERN) % 2
                    wait_tiles(dve, inv_done[0], t + 1)
                    dve.tensor_scalar(acc_tile(t), acc_tile(t), moments[:, 0, n, 0:1], inv_std[:, 0, n:n + 1],
                                      ALU.subtract, ALU.mult).then_inc(x1_done, 1)
                    wait_tiles(dve, x1_done, t + 1)
                    dve.tensor_scalar(prob_sum[:, n, :], acc_tile(t), -TH_X, None, ALU.is_lt
                                      ).then_inc(below_done, 1)
                if runs(k, OUT):
                    t = k - OUT
                    wait_tiles(dve, ffn_done, t + 1)
                    dve.scalar_tensor_tensor(out=acc_tile(t), in0=ot_ps[(e - OUT) % 2][:, :], scalar=SC_X,
                                             in1=acc_tile(t),
                                             op0=ALU.mult, op1=ALU.add).then_inc(x2_done, 1)
                if runs(k, TERN):
                    t, n = k - TERN, (e - TERN) % 2
                    wait_tiles(dve, below_done, t + 1)
                    wait_tiles(dve, tern_t_full, t - 1)
                    dve.scalar_tensor_tensor(out=prob[:, n, :], in0=acc_tile(t), scalar=TH_X,
                                             in1=prob_sum[:, n, :], op0=ALU.is_gt, op1=ALU.subtract
                                             ).then_inc(tern_done, 1)
                if runs(k, OUT):
                    t = k - OUT
                    wait_tiles(dve, x2_done, t + 1)
                    moments_of(1, t, e - OUT, acc_tile(t))

            dve.wait_ge(acc_done, NG * TT)
            over_tiles(dve, step)

        @block.tensor
        def _(pe):
            pe.wait_ge(ident_in, 16)

            def one(g, plan):
                def values(u):
                    b, s, j = unit_of(u)
                    k = b * NT + s
                    wait(pe, prob_hi_done, g, BODY, u + 1)
                    if j == 0:
                        wait(pe, o_raw_done, g, 2 * NT, k - 1)
                    pe.matmul(ot_ps[k % 2][:, :], v_sb[:, b % 2, j, :], prob_hi[:, u % 2, :], start=(j == 0), stop=False)
                    wait(pe, prob_lo_done, g, BODY, u + 1)
                    pe.matmul(ot_ps[k % 2][:, :], v_sb[:, b % 2, j, :], prob_lo[:, u % 2, :], start=False, stop=(j == s)
                              ).then_inc(pv_done, 1)

                def events(some):
                    for e in some:
                        if e[0] in X_KINDS:
                            wait_x_free(pe, plan, g, e)
                            bank = x_bank(plan, e)
                        if e[0] == "norm":
                            t = e[1]
                            pe.wait_ge(xn_done, t + 1)
                            for k in range(KC):
                                mm = pe.transpose(bank[:, k * P:(k + 1) * P], prob[:, t % 3, k * P:(k + 1) * P],
                                                  ident[:, :])
                            mm.then_inc(x_full, 1)
                        elif e[0] == "mx":
                            _, b, s, h, c = e
                            n = b * CHUNKS + chunk_index(s, h, c)
                            t0, tiles = row_chunks(s)[c]
                            wait(pe, qt_done, g, 2 * NT, b * NT + s + 1)
                            wait(pe, kt_done, g, 2 * NT, b * NT + t0 + tiles)
                            pe.matmul(bank[:, 0:tiles * P], q_t[:, h, s * P:(s + 1) * P],
                                      k_t[:, b % 2, 0, t0 * P:(t0 + tiles) * P], start=True, stop=True
                                      ).then_inc(x_full, 1)
                        elif e[0] == "mr":
                            _, b, s = e
                            wait(pe, neg_max_done, g, 2 * NT, b * NT + s + 1)
                            if plan is first:
                                pe.wait_ge(consts_cast, 1)
                            for h in range(HG):
                                mm = pe.matmul(bank[0:1, h * P:(h + 1) * P], neg_max_r[:, h:h + 1], ident_r[:, :],
                                               start=True, stop=True)
                            mm.then_inc(x_full, 1)
                        elif e[0] == "w":
                            wait(pe, win_in, g, 48, 96)
                            for a in range(3):
                                mm = pe.transpose(bank[:, a * P:(a + 1) * P], raw[:, a, e[1] * P:(e[1] + 1) * P],
                                                  ident[:, :])
                            mm.then_inc(x_full, 1)
                        elif e[0] == "wo":
                            wait(pe, wout_in, g, 16, 16)
                            for a in range(KC):
                                mm = pe.transpose(bank[:, a * P:(a + 1) * P], wout_raw[:, a, e[1] * P:(e[1] + 1) * P],
                                                  ident[:, :])
                            mm.then_inc(x_full, 1)
                        elif e[0] == "qkv":
                            _, b, t = e
                            wait(pe, win_done, g, 4, 8 if b == 2 else 4)
                            tile = (b % 2) * NT + t
                            if plan is first:
                                pe.wait_ge(y_lo_done, tile + 1)
                            for k in range(KC):
                                for n, (y, w) in enumerate(((yt_hi, win_hi), (yt_hi, win_lo), (yt_lo, win_hi))):
                                    mm = pe.matmul(bank[:, 0:WC], y[:, k, tile * P:(tile + 1) * P], w[:, k, :],
                                                   start=(k == 0 and n == 0), stop=(k == KC - 1 and n == 2))
                            mm.then_inc(x_full, 1)
                        elif e[0] == "fw":
                            pe.wait_ge(ffn_w_done, e[1] + 1)
                            for a in range(KC):
                                mm = pe.transpose(bank[:, a * P:(a + 1) * P], raw[:, 2, a * P:(a + 1) * P],
                                                  ident[:, :])
                            mm.then_inc(x_full, 1)
                        elif e[0] in ("qt", "kt"):
                            _, b, t = e
                            wait(pe, stack_done, g, 4 * NT, 2 * (b * NT + t + 1))
                            for n, a in enumerate(range(HG) if e[0] == "qt" else (HG, HG + 1)):
                                mm = pe.transpose(bank[:, n * P:(n + 1) * P], stack[:, a, :].bitcast(F32), ident[:, :])
                            mm.then_inc(x_full, 1)
                        elif e[0] == "os":
                            _, b, s = e
                            wait(pe, sum_done, g, BODY, b * UNITS + first_unit(s + 1))
                            for h in range(HG):
                                mm = pe.matmul(bank[:, h:h + 1], prob_sum[:, (b * NT + s) % 2, h * P:(h + 1) * P],
                                               ones[:, :], start=True, stop=True)
                            mm.then_inc(x_full, 1)
                        elif e[0] == "ob":
                            _, b, s = e
                            wait(pe, recip_done, g, 2 * NT, b * NT + s + 1)
                            for h in range(HG):
                                c, a = divmod(h, 2)
                                mm = pe.matmul(bank[a * DH:(a + 1) * DH, c * P:(c + 1) * P],
                                               recip[:, h:h + 1].to_broadcast([P, DH]), ident[:, :],
                                               start=True, stop=True)
                            mm.then_inc(x_full, 1)
                        elif e[0] == "op":
                            _, b, s = e
                            wait(pe, wout_done, g, 2, 2 if b >= 0 else 0)
                            wait(pe, o_hi_done, g, 2 * NT, b * NT + s + 1)
                            wait(pe, o_lo_done, g, 2 * NT, b * NT + s + 1)
                            for c in range(2):
                                for n, (o, w) in enumerate(((o_hi, wout_hi), (o_hi, wout_lo), (o_lo, wout_hi))):
                                    mm = pe.matmul(bank[:, :], o[:, c, :], w[:, c, :], start=(c == 0 and n == 0),
                                                   stop=(c == 1 and n == 2))
                            mm.then_inc(x_full, 1)

                if plan is opening:
                    pe.wait_ge(y_lo_done, TT)
                    pe.wait_ge(consts_cast, 2)
                    pe.wait_ge(consts_set, 5)
                for u in range(len(plan.ahead)):
                    if u < plan.units:
                        b, s, j = unit_of(u)
                        k = (b * NT + s) % 2
                        if j == 0:
                            wait(pe, q_shift_in[k], g, 16 * NT, 16 * ((b * NT + s) // 2 + 1))
                            wait(pe, shift_done, g, 2 * NT, b * NT + s + 1)
                            wait(pe, v_done, g, 2 * NT, b * NT + s + 1)
                        wait(pe, prob_done, g, BODY, u - 1)
                        bank = st_ps[u % 2]
                        keys = k_t[:, b, :, j * P:(j + 1) * P]
                        pe.matmul(bank[:, :], keys[:, 0], q_tile(s), start=True, stop=False)
                        mm = pe.matmul(bank[:, :], keys[0:DH + 1, 1], q_shift[0:DH + 1, k, :, :], start=False,
                                       stop=(j < s))
                        if j == s:
                            mm = pe.matmul(bank[:, :], ident_r[:, :],
                                           trit_r[:, :].unsqueeze(1).to_broadcast([P, HG, P]), start=False, stop=True)
                        mm.then_inc(st_done, 1)
                    events(plan.ahead[u])
                    events(plan.behind[u])
                    if 0 < u <= plan.units or u == 0 and plan in (body, final):
                        values(u - 1)

            over_bodies(pe, one)

            def step(k, e):
                if runs(k, FFN):
                    t, n = k - FFN, (e - FFN) % 2
                    wait_tiles(pe, xq_done, t + 1)
                    wait_tiles(pe, x2_done, t - 1)
                    for c in range(KC):
                        for w in (ffn_hi, ffn_lo):
                            mm = pe.matmul(ot_ps[n][:, :], xq_t[:, n, c, :], w[:, c, :], start=(c == 0 and w is ffn_hi),
                                           stop=(c == KC - 1 and w is ffn_lo))
                    mm.then_inc(ffn_done, 1)
                if runs(k, TERN):
                    t, n = k - TERN, (e - TERN) % 2
                    wait_tiles(pe, tern_done, t + 1)
                    wait_tiles(pe, xq_done, t - 1)
                    for c in range(KC):
                        mm = pe.transpose(x_ps[n][:, c * P:(c + 1) * P], prob[:, n, c * P:(c + 1) * P], ident[:, :])
                    mm.then_inc(tern_t_full, 1)

            pe.wait_ge(ffn_lo_done, KC)
            over_tiles(pe, step)


_INS = ["L0_attn_x", "L0_attn_w_in", "L0_attn_w_out", "L0_attn_rms_w", "L0_ffn_weight", "L0_ffn_rram_variation"]


def shape_constants(seq):
    import numpy as np

    f = np.float32
    exponent = np.arange(0, DH, 2, dtype=f) / f(DH)
    inv_freq = f(1) / (ROPE_THETA ** exponent.astype(np.float64)).astype(f)
    angle = (np.arange(seq, dtype=f)[:, None] * inv_freq[None, :]).astype(np.float64)
    cos, sin = np.cos(angle).astype(f), np.sin(angle).astype(f)
    later = np.triu(np.full((P, P), MASKED, f), 1)
    return {
        "cos_dram": np.concatenate([cos, cos], 1), "sin_dram": np.concatenate([-sin, sin], 1),
        "ident_dram": np.eye(P, dtype=f), "tri_dram": later, "trit_dram": np.ascontiguousarray(later.T),
    }


def kernel(**inputs):
    import numpy as np
    import concourse.bacc as bacc
    from concourse.bass_utils import run_bass_kernel_spmd as run

    nc = bacc.Bacc("TRN2", target_bir_lowering=False, num_devices=1)
    arrays = {name: np.ascontiguousarray(inputs[name]) for name in _INS}
    shape = arrays["L0_attn_x"].shape
    arrays["L0_attn_rms_w"] = np.ascontiguousarray(arrays["L0_attn_rms_w"].reshape(-1, P).T)
    arrays.update(shape_constants(shape[1]))
    args = [nc.dram_tensor(n, a.shape, mybir.dt.from_np(a.dtype), kind="ExternalInput").ap() for n, a in arrays.items()]
    args.append(nc.dram_tensor("out", shape, F32, kind="ExternalOutput").ap())
    seq_block(nc, *args)
    return run(nc, [arrays], core_ids=[0]).results[0]["out"]
```

```python
from contextlib import ExitStack

import concourse.bass as bass
from concourse import mybir

F32 = mybir.dt.float32
F32R = mybir.dt.float32r
BF16 = mybir.dt.bfloat16
ALU = mybir.AluOpType
ACT = mybir.ActivationFunctionType
AX_X = mybir.AxisListType.X

P = 128
DH = 64
NG = 8
HG = 4
BANK = 512
MASKED = -1e30
ROPE_THETA = 10000.0
RMS_EPS = 1e-6
LN_EPS = 1e-5
TH_X, SC_X = 0.33, 0.5
TH_W, SC_W = 0.2, 0.6

NT = 8
UNITS = NT * (NT + 1) // 2
BODY = 2 * UNITS
CHUNKS = sum(HG * (1 + (s >= 4)) for s in range(NT))
X_KINDS = ("mx", "mr", "qkv", "qt", "kt", "os", "ob", "op", "w", "wo", "fw", "norm", "tern", "ffn")
RING = 4
CARRIED = 2


def first_unit(s):
    return s * (s + 1) // 2


def row_chunks(s):
    return [(0, s + 1)] if s < 4 else [(0, 4), (4, s - 3)]


def chunk_index(s, h, c):
    return sum(HG * len(row_chunks(r)) for r in range(s)) + h * len(row_chunks(s)) + c


class Plan:

    def __init__(self, slots, units):
        self.units = units
        self.ahead = [[] for _ in range(slots)]
        self.behind = [[] for _ in range(slots)]

    def number(self):
        self.x = {}
        for u in range(len(self.ahead)):
            for e in self.ahead[u] + self.behind[u]:
                if e[0] in X_KINDS:
                    self.x[e] = len(self.x)
        self.uses = -(-len(self.x) // RING) * RING
        return self


MAXIMA = (
    (0, 0, 1), (1, 3, 4), (4, 7, 8), (9, 12, 13), (13, 18, 19), (20, 25, 26), (29, 33, 33), (33, 34, 35),
    (35, 36, 37), (38, 39, 40), (40, 43, 44), (45, 48, 49), (49, 52, 55), (55, 60, 62), (65, 68, 69), (70, 70, 71)
)
PROJECT = (
    (0, 5, 5), (7, 9, 10), (10, 12, 13), (14, 18, 18), (20, 23, 25), (25, 28, 28), (29, 32, 32), (32, 35, 37),
    (36, 39, 39), (42, 45, 46), (46, 48, 50), (50, 53, 53), (54, 57, 58), (59, 62, 63), (63, 66, 67), (67, 70, 71)
)
W_OUT = (5, 5)
W_IN = (43, 43, 44, 44)
FFN_IN = (44, 46, 48, 51)
EARLY = (
    (51, 52, 53, 55, 56, 57), (55, 56, 57, 59, 60, 61), (57, 58, 59, 61, 62, 63), (58, 59, 61, 62, 63, 64),
    (61, 62, 63, 64, 66, 67), (62, 64, 65, 67, 68, 69), (64, 65, 66, 68, 69, 71), (66, 67, 68, 70, 71, 72)
)
OUTPUT = (
    (2, 2, 3, 4, 5), (4, 3, 4, 5, 6), (2, 2, 3, 4, 5), (2, 2, 3, 4, 6), (2, 2, 3, 4, 6), (2, 2, 4, 5, 8),
    (2, 2, 3, 4, 5), (2, 2, 4, 4, 7), (2, 2, 3, 4, 5), (2, 2, 3, 4, 5), (2, 2, 3, 3, 5), (2, 2, 3, 4, 6),
    (2, 2, 3, 4, 5), (2, 2, 5, 5, 7), (2, 2, 3, 4, 9), (3, 1, 4, 6, 8), (3, 2, 3, 4, 5)
)


def body_plan(opening, last):
    plan = Plan(BODY + (7 if last else 0), BODY)
    for b, s in [(0, s) for s in range(2, NT)] + [(1, s) for s in range(NT)] + [(2, 0), (2, 1)]:
        if last and b == 2:
            continue
        chunks = [(h, c) for h in range(HG) for c in range(len(row_chunks(s)))]
        lo, hi, row = MAXIMA[b * NT + s - 2]
        for n, (h, c) in enumerate(chunks):
            plan.ahead[lo + (hi - lo + 1) * n // len(chunks)].append(("mx", b, s, h, c))
        plan.ahead[row].append(("mr", b, s))
    for n, (u, qt, kt) in enumerate(PROJECT):
        b, t = divmod(n + NT - CARRIED, NT)
        if not last or b < 2:
            plan.behind[u].append(("qkv", b, t))
            plan.behind[qt].append(("qt", b, t))
            plan.behind[kt].append(("kt", b, t))
    for c, u in enumerate(W_OUT):
        plan.behind[u].append(("wo", c))
    if not last:
        for c, u in enumerate(W_IN):
            plan.behind[u].append(("w", c))
    else:
        for n in range(4):
            plan.behind[FFN_IN[n]].append(("fw", n))
        for t in range(NT):
            for kind, u in zip(("ln", "x1", "tern", "ffn", "res", "out"), EARLY[t]):
                (plan.ahead if kind == "res" else plan.behind)[u].append((kind, t))
    for b, s in [(-1, NT - 1)] + [(b, s) for b in range(2) for s in range(NT)]:
        end = b * UNITS + first_unit(s + 1) - 1
        if (b, s) == (-1, NT - 1) and opening or (b, s) == (1, NT - 1) and not last:
            continue
        for kind, lag in zip(("oe", "os", "ob", "oh", "op"), OUTPUT[b * NT + s + 1]):
            plan.behind[end + lag].append((kind, b, s))
    return plan.number()


def first_plan():
    norm = [("sq", 0), ("xn", 0), ("xn", 1)]
    for t in range(2 * NT):
        if t + 2 < 2 * NT:
            if (t + 2) % 4 == 0:
                norm.append(("sq", (t + 2) // 4))
            norm.append(("xn", t + 2))
        norm.append(("norm", t))
    rest = [("consts",)] + [("w", c) for c in range(4)]
    for t in range(NT - CARRIED + 1):
        if t < NT - CARRIED:
            rest.append(("qkv", 2, t))
        if t:
            rest += [("qt", 2, t - 1), ("kt", 2, t - 1)]
        if t in (2, 4):
            rest += [("mx", 2, t // 2 - 1, h, 0) for h in range(HG)]
        if t in (3, 5):
            rest.append(("mr", 2, (t - 3) // 2))
    start = norm.index(("norm", 3)) + 1
    order = norm[:start]
    norm = norm[start:]
    done = 0
    for n, e in enumerate(rest):
        order.append(e)
        upto = len(norm) * (n + 1) // len(rest)
        order += norm[done:upto]
        done = upto
    plan = Plan(1, 0)
    plan.ahead[0] = order
    return plan.number()


def seq_block(nc, x, w_in, w_out, rms_w, ffn_w, ffn_r, cos, sin, ident_d, tri_d, trit_d, out):
    B, S, D = x.shape
    TT = B * S // P
    KC = D // P
    QC = HG * DH
    WC = QC + 2 * DH
    NQ = NG * QC
    assert B == 2 and S == NT * P and D == BANK and WC <= BANK
    LAST = NG - 1

    first, opening = first_plan(), body_plan(True, False)
    body, final = body_plan(False, False), body_plan(False, True)
    first.base = 0, 0
    opening.base = first.uses, len(first.x)
    body.base = final.base = (opening.base[0] + opening.uses - body.uses,
                              opening.base[1] + len(opening.x) - len(body.x))
    opening.past, body.past, final.past = first, body, body
    assert list(body.x)[-2 * RING:] == list(opening.x)[-2 * RING:]

    x_v = x.rearrange("b (t p) d -> p (b t) d", p=P)
    out_v = out.rearrange("b (t p) d -> p (b t) d", p=P)

    with ExitStack() as ctx:
        def sb(name, shape, dt=F32):
            return ctx.enter_context(nc.sbuf_tensor(name, shape, dt))

        def ps(name):
            return ctx.enter_context(nc.psum_tensor(name, [P, BANK], F32))

        def sem(name):
            return ctx.enter_context(nc.semaphore(name))

        acc = sb("acc", [P, TT, D])
        yt_hi = sb("yt_hi", [P, KC, TT * P], F32R)
        yt_lo = sb("yt_lo", [P, KC, TT * P], F32R)
        ffn_hi = yt_hi[:, :, 0:D]
        ffn_lo = yt_lo[:, :, 0:D]
        cos_sb = sb("cos_sb", [P, NT, DH])
        sin_sb = sb("sin_sb", [P, NT, DH])
        ident = sb("ident", [P, P])
        ident_r = sb("ident_r", [P, P], F32R)
        trit_r = sb("trit_r", [P, P], F32R)
        mask = sb("mask", [P, BANK])
        ones = sb("ones", [P, 1])
        rms = sb("rms", [P, KC])
        ss = sb("ss", [P, TT])
        rstd = sb("rstd", [P, TT])
        neg_half = sb("neg_half", [P, TT])
        raw = sb("raw", [P, 3, D])
        wout_raw = raw[:, 0:2, :].rearrange("p a (b c) -> p (a b) c", b=2)
        win_hi = sb("win_hi", [P, KC, WC], F32R)
        win_lo = sb("win_lo", [P, KC, WC], F32R)
        wout_hi = sb("wout_hi", [P, 2, D], F32R)
        wout_lo = sb("wout_lo", [P, 2, D], F32R)
        rope_a = sb("rope_a", [P, HG + 1, DH])
        rope_b = sb("rope_b", [P, HG + 1, DH])
        roped = sb("roped", [P, HG + 1, DH])
        stack = sb("stack", [P, HG + 2, P], F32R)
        q_t = sb("q_t", [P, HG, S], F32R)
        k_t = sb("k_t", [P, 2, 2, S], F32R)
        v_sb = sb("v_sb", [P, 2, NT, P], F32R)
        q_shift = sb("q_shift", [P, 2, HG, P], F32R)
        neg_max = sb("neg_max", [P, HG])
        row_max = sb("row_max", [P, HG])
        neg_max_r = sb("neg_max_r", [P, HG], F32R)
        junk = sb("junk", [P, 2, BANK], BF16)
        prob = sb("prob", [P, 3, BANK])
        prob_hi = sb("prob_hi", [P, 2, BANK], F32R)
        prob_lo = sb("prob_lo", [P, 2, BANK], F32R)
        prob_sum = sb("prob_sum", [P, 2, BANK])
        o_low = sb("o_low", [DH, BANK])
        o_raw = sb("o_raw", [P, 2, P])
        recip = sb("recip", [P, HG])
        o_t = sb("o_t", [P, 2, P])
        o_hi = sb("o_hi", [P, 2, P], F32R)
        o_lo = sb("o_lo", [P, 2, P], F32R)
        stats = sb("stats", [P, 2, 4, 6])
        moments = sb("moments", [P, 2, 4, 2])
        inv_std = sb("inv_std", [P, 2, 4])
        shift = sb("shift", [P, 4])

        st_ps = [ps("st0"), ps("st1")]
        ot_ps = [ps("ot0"), ps("ot1")]
        x_ps = [ps(f"x{n}") for n in range(RING)]

        waited = sem("waited")
        ident_in = sem("ident_in")
        rms_in = sem("rms_in")
        consts_in = sem("consts_in")
        x_in = [sem(f"x_in{n}") for n in range(4)]
        ffn_in = [sem(f"ffn_in{n}") for n in range(2)]
        win_in = sem("win_in")
        wout_in = sem("wout_in")
        consts_set = sem("consts_set")
        consts_cast = sem("consts_cast")
        ss_done = sem("ss_done")
        rstd_mid = sem("rstd_mid")
        rstd_done = sem("rstd_done")
        xn_done = sem("xn_done")
        y_hi_done = sem("y_hi_done")
        y_lo_done = sem("y_lo_done")
        tern_step = sem("tern_step")
        ffn_w_done = sem("ffn_w_done")
        ffn_hi_done = sem("ffn_hi_done")
        ffn_lo_done = sem("ffn_lo_done")
        doubled = sem("doubled")

        x_full = sem("x_full")
        win_hi_done = sem("win_hi_done")
        win_done = sem("win_done")
        wout_hi_done = sem("wout_hi_done")
        wout_done = sem("wout_done")
        roped_ab = sem("roped_ab")
        rope_sum = sem("rope_sum")
        stack_hi = sem("stack_hi")
        stack_done = sem("stack_done")
        v_hi_done = sem("v_hi_done")
        v_done = sem("v_done")
        qt_done = sem("qt_done")
        kt_done = sem("kt_done")
        q_shift_in = [sem(f"q_shift_in{n}") for n in range(2)]
        mx_done = sem("mx_done")
        neg_max_done = sem("neg_max_done")
        shift_done = sem("shift_done")
        st_done = sem("st_done")
        prob_done = sem("prob_done")
        prob_hi_done = sem("prob_hi_done")
        prob_lo_done = sem("prob_lo_done")
        sum_done = sem("sum_done")
        pv_done = sem("pv_done")
        o_low_done = sem("o_low_done")
        o_raw_done = sem("o_raw_done")
        recip_done = sem("recip_done")
        o_t_done = sem("o_t_done")
        o_hi_done = sem("o_hi_done")
        o_lo_done = sem("o_lo_done")
        acc_done = sem("acc_done")

        stat_done = [sem(f"stat_done{n}") for n in (1, 2)]
        var_done = [sem(f"var_done{n}") for n in (1, 2)]
        inv_step = [sem(f"inv_step{n}") for n in (1, 2)]
        inv_done = [sem(f"inv_done{n}") for n in (1, 2)]
        x1_done = sem("x1_done")
        below_done = sem("below_done")
        tern_done = sem("tern_done")
        tern_t_full = sem("tern_t_full")
        xq_done = sem("xq_done")
        ffn_done = sem("ffn_done")
        x2_done = sem("x2_done")
        out_done = sem("out_done")
        stored = sem("stored")

        block = ctx.enter_context(nc.Block())

        met_counts = {}

        def wait(eng, s, g, per_body, count):
            if met_counts.get((eng, s), count - 1) >= count:
                return
            met_counts[eng, s] = count
            if isinstance(g, int):
                if g * per_body + count > 0:
                    eng.wait_ge(s, g * per_body + count)
            else:
                assert per_body + count > 0
                eng.wait_ge(s, g * per_body + count)

        def met(eng):
            eng.sem_inc(waited, 1)

        def x_bank(plan, e):
            return x_ps[(plan.base[0] + plan.x[e]) % RING]

        def wait_x_full(eng, plan, g, e):
            bodies = 0 if plan is first or plan is opening else g
            wait(eng, x_full, bodies, len(body.x), plan.base[1] + plan.x[e] + 1)
            return x_bank(plan, e)

        def wait_x_free(eng, plan, g, e):
            n, past, back = plan.x[e] - RING, plan, 0
            if n < 0:
                if plan is first:
                    return
                past, back = plan.past, 2
                n += past.uses
                while n >= len(past.x):
                    n -= RING
            kind, *what = list(past.x)[n]
            tile = (what[0] - back) * NT + what[1] + 1 if len(what) >= 2 else 0
            assert len(what) >= 2 or not back or kind == "norm"
            if kind == "mx":
                wait(eng, mx_done, g, 2 * CHUNKS, (what[0] - back) * CHUNKS + chunk_index(*what[1:]) + 1)
            elif kind == "mr":
                wait(eng, shift_done, g, 2 * NT, tile)
            elif kind == "qkv":
                wait(eng, v_done, g, 2 * NT, tile)
            elif kind == "qt":
                wait(eng, qt_done, g, 2 * NT, tile)
            elif kind == "kt":
                wait(eng, kt_done, g, 2 * NT, tile)
            elif kind == "os":
                wait(eng, recip_done, g, 2 * NT, tile)
            elif kind == "ob":
                wait(eng, o_t_done, g, 2 * NT, tile)
            elif kind == "op":
                wait(eng, acc_done, g, 2 * NT, tile)
            elif kind == "norm":
                eng.wait_ge(y_lo_done, what[0] + 1)
            elif kind == "w":
                wait(eng, win_done, g, 4, 4 + what[0] + 1)
            elif kind == "wo":
                wait(eng, wout_done, g, 2, what[0] + 1)
            elif kind == "fw":
                eng.wait_ge(ffn_lo_done, what[0] + 1)
            elif kind == "tern":
                eng.wait_ge(xq_done, what[0] + 1)
            elif kind == "ffn":
                eng.wait_ge(x2_done, what[0] + 1)

        def unit_of(u):
            b, u = divmod(u, UNITS)
            s = max(s for s in range(NT) if first_unit(s) <= u)
            return b, s, u - first_unit(s)

        def over_bodies(eng, one):
            one(-1, first)
            met_counts.clear()
            one(0, opening)
            met_counts.clear()
            with eng.Fori(1, LAST) as g:
                one(g, body)
            met_counts.clear()
            one(LAST, final)

        LN, TERN, FFN, OUT = 0, 2, 3, 4
        LATE = range(NT, TT + OUT)

        def runs(k, lag):
            return NT <= k - lag < TT

        def below_tile(t):
            return raw[:, 0, :] if t < NT else prob_sum[:, t % 2, :]

        def tern_tile(t):
            return raw[:, 1, :] if t < NT else prob[:, t % 2, :]

        def xq_tile(t):
            return yt_hi[:, :, D + (t % 2) * P:D + (t % 2 + 1) * P]

        def q_tile(t):
            return q_t[:, :, t * P:(t + 1) * P]

        @block.sync
        def _(sp):
            def load_x(n):
                sp.dma_start(acc[:, 4 * n:4 * n + 4, :], x_v[:, 4 * n:4 * n + 4, :]).then_inc(x_in[n], 16)

            def load_win(g):
                sp.dma_start(raw[:, 0:2, :], w_in[bass.ds(g * QC, QC), :].rearrange("(a p) d -> p a d", p=P)
                             ).then_inc(win_in, 16)
                sp.dma_start(raw[0:DH, 2, :], w_in[bass.ds(g * DH + NQ, DH), :]).then_inc(win_in, 16)
                sp.dma_start(raw[DH:P, 2, :], w_in[bass.ds(g * DH + (NQ + NG * DH), DH), :]
                             ).then_inc(win_in, 16)

            def load_wout(g):
                sp.dma_start(wout_raw[:, :, :], w_out[:, bass.ds(g * QC, QC)].rearrange("(a p) c -> p a c", p=P)
                             ).then_inc(wout_in, 16)

            load_x(0)
            sp.dma_start(ident[:, :], ident_d).then_inc(ident_in, 16)
            load_win(0)
            sp.dma_start(rms[:, :], rms_w).then_inc(rms_in, 16)
            sp.dma_start(mask[:, BANK - P:BANK], tri_d).then_inc(consts_in, 16)
            sp.dma_start(prob_sum[:, 0, 0:P], trit_d).then_inc(consts_in, 16)
            sp.dma_start(cos_sb[:, :, :], cos.rearrange("(t p) d -> p t d", p=P)).then_inc(consts_in, 16)
            sp.dma_start(sin_sb[:, :, :], sin.rearrange("(t p) d -> p t d", p=P)).then_inc(consts_in, 16)
            for n in range(1, 4):
                load_x(n)

            def store(t):
                sp.wait_ge(out_done, t + 1)
                sp.dma_start(out_v[:, t, :], acc[:, t, :]).then_inc(stored, 16)

            def one(g, plan):
                for u in range(len(plan.ahead)):
                    for e in plan.ahead[u] + plan.behind[u]:
                        if e[0] == "mr":
                            _, b, s = e
                            wait(sp, qt_done, g, 2 * NT, b * NT + s + 1)
                            met(sp)
                            k = (b * NT + s) % 2
                            b0, s0 = divmod(b * NT + s - 2, NT)
                            wait(sp, st_done, g, BODY, b0 * UNITS + first_unit(s0 + 1))
                            sp.dma_start(q_shift[0:DH, k, :, :].bitcast(F32), q_tile(s)[0:DH, :, :].bitcast(F32)
                                         ).then_inc(q_shift_in[k], 16)
                        elif e == ("wo", 1) and plan is not final:
                            wait(sp, wout_done, g, 2, 2)
                            met(sp)
                            load_win(g + 1)
                        elif e == ("w", 3):
                            wait(sp, win_done, g, 4, 8)
                            met(sp)
                            load_wout(g + 1)
                        elif e[0] == "out":
                            store(e[1])
                        elif e[0] == "fw":
                            n = e[1]
                            sp.wait_ge(wout_done, 2 * NG)
                            if n:
                                sp.wait_ge(ffn_lo_done, n)
                            sp.dma_start(raw[:, 0, :], ffn_w[n * P:(n + 1) * P, :]).then_inc(ffn_in[0], 16)
                            sp.dma_start(raw[:, 1, :], ffn_r[n * P:(n + 1) * P, :]).then_inc(ffn_in[1], 16)

            over_bodies(sp, one)

            for t in range(NT, TT):
                store(t)
            sp.wait_ge(stored, 16 * TT)

        @block.gpsimd
        def _(pool):
            pool.memset(neg_half[:, :], -0.5).then_inc(consts_set, 1)
            pool.memset(ones[:, :], 1.0).then_inc(consts_set, 1)
            pool.memset(mask[:, 0:BANK - P], 0.0).then_inc(consts_set, 1)
            pool.memset(stack[:, HG + 1, :].bitcast(F32), 0.0).then_inc(consts_set, 1)
            pool.wait_ge(consts_set, 4)
            pool.memset(stack[:, HG + 1, DH:DH + 1].bitcast(F32), 1.0).then_inc(consts_set, 1)
            def inverse_std(n, t):
                inv = inv_std[:, n, t % 4:t % 4 + 1]
                pool.wait_ge(var_done[n], t + 1)
                pool.tensor_scalar(inv, moments[:, n, t % 4, 1:2], 1.0, LN_EPS, ALU.mult, ALU.add
                                   ).then_inc(inv_step[n], 1)
                pool.wait_ge(inv_step[n], t + 1)
                pool.tensor_tensor(inv, inv, neg_half[:, 0:1], ALU.pow).then_inc(inv_done[n], 1)
                if n == 1:
                    pool.wait_ge(inv_done[n], t * 2 + 1)
                    pool.tensor_scalar(shift[:, t % 4:t % 4 + 1], moments[:, n, t % 4, 0:1], inv, -1.0,
                                       ALU.mult, ALU.mult).then_inc(inv_done[n], 1)

            def one(g, plan):
                for u in range(len(plan.ahead)):
                    if u < plan.units:
                        b, s, j = unit_of(u)
                        k = b * NT + s
                        total = prob_sum[:, k % 2, :]
                        if s == 0:
                            wait(pool, recip_done, g, 2 * NT, k - 1)
                            wait(pool, prob_done, g, BODY, u + 1)
                            met(pool)
                            pool.tensor_scalar(total, prob[:, u % 3, :], 1.0, None, ALU.mult).then_inc(sum_done, 1)
                        elif j:
                            if j == 1:
                                wait(pool, recip_done, g, 2 * NT, k - 1)
                            else:
                                wait(pool, sum_done, g, BODY, u)
                            wait(pool, prob_done, g, BODY, u + 1)
                            pool.tensor_tensor(total, prob[:, (u - 1) % 3, :] if j == 1 else total,
                                               prob[:, u % 3, :], ALU.add).then_inc(sum_done, 2 if j == 1 else 1)
                    for e in plan.ahead[u] + plan.behind[u]:
                        if e[0] in ("ln", "res"):
                            inverse_std(("ln", "res").index(e[0]), e[1])
                        elif e[0] == "sq":
                            n = e[1]
                            some = slice(4 * n, 4 * n + 4)
                            pool.wait_ge(ss_done, 4 * n + 4)
                            pool.tensor_scalar(rstd[:, some], ss[:, some], 1.0 / D, RMS_EPS, ALU.mult, ALU.add
                                               ).then_inc(rstd_mid, 1)
                            pool.wait_ge(rstd_mid, n + 1)
                            pool.tensor_tensor(rstd[:, some], rstd[:, some], neg_half[:, some], ALU.pow
                                               ).then_inc(rstd_done, 1)
                        elif e[0] == "qkv":
                            _, b, t = e
                            n = b * NT + t
                            wait(pool, roped_ab, g, 2 * NT, n + 1)
                            wait(pool, kt_done, g, 2 * NT, n)
                            pool.tensor_tensor(roped[:, :, :], rope_a[:, :, :], rope_b[:, :, :], ALU.add
                                               ).then_inc(rope_sum, 1)
                            pool.tensor_tensor(stack[:, 0:HG + 1, 0:DH], rope_a[:, :, :], rope_b[:, :, :], ALU.add
                                               ).then_inc(stack_hi, 1)
                            wait(pool, rope_sum, g, 2 * NT, n + 1)
                            met(pool)
                            pool.tensor_scalar(stack[:, HG, DH:P], roped[:, HG, :], 1.0, None, ALU.mult
                                               ).then_inc(stack_hi, 1)
                            wait(pool, stack_hi, g, 4 * NT, 2 * n + 2)
                            pool.tensor_tensor(stack[:, 0:HG, DH:P], roped[:, 0:HG, :],
                                               stack[:, 0:HG, 0:DH].bitcast(F32), ALU.subtract).then_inc(stack_done, 1)
                            pool.tensor_tensor(stack[:, HG + 1, 0:DH], roped[:, HG, :],
                                               stack[:, HG, 0:DH].bitcast(F32), ALU.subtract).then_inc(stack_done, 1)

            over_bodies(pool, one)

            for k in LATE:
                if runs(k, OUT):
                    inverse_std(1, k - OUT)
                if runs(k, LN):
                    inverse_std(0, k - LN)

        @block.scalar
        def _(act):
            def move_ternary(t, bank):
                if t >= 2:
                    act.wait_ge(x2_done, t - 1)
                act.activation(xq_tile(t), bank[:, :].rearrange("p (k q) -> p k q", k=KC), ACT.Copy
                               ).then_inc(xq_done, 1)

            def result(t):
                act.wait_ge(inv_done[1], t * 2 + 2)
                act.activation(acc[:, t, :], acc[:, t, :], ACT.Identity, bias=shift[:, t % 4:t % 4 + 1],
                               scale=inv_std[:, 1, t % 4:t % 4 + 1]).then_inc(out_done, 1)

            def one(g, plan):
                for u in range(len(plan.ahead)):
                    if u < plan.units:
                        wait(act, st_done, g, BODY, u + 1)
                        wait(act, prob_lo_done, g, BODY, u - 2)
                        wait(act, sum_done, g, BODY, u - 2)
                        act.activation(prob[:, u % 3, :], st_ps[u % 2][:, :], ACT.Exp, scale=DH ** -0.5
                                       ).then_inc(prob_done, 1)
                        wait(act, pv_done, g, BODY, u - 1)
                        act.activation(prob_hi[:, u % 2, :], st_ps[u % 2][:, :], ACT.Exp, scale=DH ** -0.5
                                       ).then_inc(prob_hi_done, 1)
                    for e in plan.ahead[u] + plan.behind[u]:
                        if e[0] == "tern":
                            move_ternary(e[1], wait_x_full(act, plan, g, e))
                        elif e[0] == "out":
                            result(e[1])
                        elif e[0] == "sq":
                            act.wait_ge(x_in[e[1]], 16)
                            for t in range(4 * e[1], 4 * e[1] + 4):
                                if t:
                                    act.wait_ge(ss_done, t)
                                act.activation(junk[:, 0, :], acc[:, t, :], ACT.Square, accum_out=ss[:, t:t + 1]
                                               ).then_inc(ss_done, 1)
                        elif e[0] == "norm":
                            t = e[1]
                            bank = wait_x_full(act, plan, g, e)
                            act.activation(yt_hi[:, :, t * P:(t + 1) * P],
                                           bank[:, :].rearrange("p (k q) -> p k q", k=KC), ACT.Copy
                                           ).then_inc(y_hi_done, 1)
                        elif e[0] == "mr":
                            _, b, s = e
                            bank = wait_x_full(act, plan, g, e)
                            b0, s0 = divmod(b * NT + s - 2, NT)
                            wait(act, st_done, g, BODY, b0 * UNITS + first_unit(s0 + 1))
                            act.activation(q_shift[DH:DH + 1, (b * NT + s) % 2, :, :],
                                           bank[0:1, :].rearrange("p (h q) -> p h q", h=HG), ACT.Copy
                                           ).then_inc(shift_done, 1)
                        elif e[0] == "w":
                            bank = wait_x_full(act, plan, g, e)
                            if plan is first:
                                act.wait_ge(rms_in, 16)
                            act.activation(win_hi[:, e[1], :], bank[:, 0:WC], ACT.Copy, scale=rms[:, e[1]:e[1] + 1]
                                           ).then_inc(win_hi_done, 1)
                        elif e[0] == "wo":
                            bank = wait_x_full(act, plan, g, e)
                            act.activation(wout_hi[:, e[1], :], bank[:, :], ACT.Copy).then_inc(wout_hi_done, 1)
                        elif e[0] == "fw":
                            bank = wait_x_full(act, plan, g, e)
                            act.activation(ffn_hi[:, :, e[1] * P:(e[1] + 1) * P],
                                           bank[:, :].rearrange("p (k q) -> p k q", k=KC), ACT.Copy
                                           ).then_inc(ffn_hi_done, 1)
                        elif e[0] == "qt":
                            _, b, t = e
                            bank = wait_x_full(act, plan, g, e)
                            wait(act, st_done, g, BODY, (b - 1) * UNITS + first_unit(t + 1))
                            act.activation(q_tile(t), bank[:, :].rearrange("p (h q) -> p h q", h=HG), ACT.Copy
                                           ).then_inc(qt_done, 1)
                        elif e[0] == "kt":
                            _, b, t = e
                            bank = wait_x_full(act, plan, g, e)
                            wait(act, st_done, g, BODY, (b - 1) * UNITS)
                            act.activation(k_t[:, b % 2, :, t * P:(t + 1) * P],
                                           bank[:, 0:2 * P].rearrange("p (a q) -> p a q", a=2), ACT.Copy
                                           ).then_inc(kt_done, 1)
                        elif e[0] == "oe":
                            _, b, s = e
                            k = b * NT + s
                            wait(act, pv_done, g, BODY, b * UNITS + first_unit(s + 1))
                            wait(act, o_raw_done, g, 2 * NT, k)
                            act.activation(o_low[:, :], ot_ps[k % 2][DH:P, :], ACT.Copy).then_inc(o_low_done, 1)
                        elif e[0] == "oh":
                            _, b, s = e
                            kk = b * NT + s
                            wait(act, o_t_done, g, 2 * NT, kk + 1)
                            wait(act, acc_done, g, 2 * NT, kk)
                            act.activation(o_hi[:, :, :], o_t[:, :, :], ACT.Copy).then_inc(o_hi_done, 1)

            over_bodies(act, one)

            for k in LATE:
                if runs(k, TERN):
                    act.wait_ge(tern_t_full, k - TERN - NT + 1)
                    move_ternary(k - TERN, x_ps[(k - TERN) % 2])
                if runs(k, OUT):
                    result(k - OUT)

        @block.vector
        def _(dve):
            def statistics(n, t):
                dve.bn_stats(stats[:, n, t % 4, :], acc[:, t, :]).then_inc(stat_done[n], 1)

            def moments_of(n, t):
                dve.wait_ge(stat_done[n], t + 1)
                dve.bn_aggr(moments[:, n, t % 4, :], stats[:, n, t % 4, :]).then_inc(var_done[n], 1)

            def first_norm(t):
                dve.wait_ge(inv_done[0], t + 1)
                dve.tensor_scalar(acc[:, t, :], acc[:, t, :], moments[:, 0, t % 4, 0:1], inv_std[:, 0, t % 4:t % 4 + 1],
                                  ALU.subtract, ALU.mult).then_inc(x1_done, 1)

            def below(t):
                dve.wait_ge(x1_done, t + 1)
                dve.tensor_scalar(below_tile(t), acc[:, t, :], -TH_X, None, ALU.is_lt).then_inc(below_done, 1)

            def ternary(t):
                dve.wait_ge(below_done, t + 1)
                buffers = 1 if t < NT else 2
                if t >= buffers:
                    dve.wait_ge(xq_done, t - buffers + 1)
                dve.scalar_tensor_tensor(out=tern_tile(t), in0=acc[:, t, :], scalar=TH_X, in1=below_tile(t),
                                         op0=ALU.is_gt, op1=ALU.subtract).then_inc(tern_done, 1)

            def residual(t, bank):
                dve.scalar_tensor_tensor(out=acc[:, t, :], in0=bank[:, :], scalar=SC_X, in1=acc[:, t, :],
                                         op0=ALU.mult, op1=ALU.add).then_inc(x2_done, 1)

            def one(g, plan):
                def events(some):
                    for e in some:
                        if e[0] == "ln":
                            dve.wait_ge(acc_done, LAST * TT + e[1] + 1)
                            statistics(0, e[1])
                            moments_of(0, e[1])
                        elif e[0] == "x1":
                            if e[1] == 0:
                                dve.wait_ge(ffn_lo_done, KC)
                            first_norm(e[1])
                            below(e[1])
                            ternary(e[1])
                        elif e[0] == "res":
                            residual(e[1], wait_x_full(dve, plan, g, ("ffn", e[1])))
                            dve.wait_ge(x2_done, e[1] + 1)
                            statistics(1, e[1])
                            moments_of(1, e[1])
                        elif e[0] == "consts":
                            dve.wait_ge(consts_in, 16 * 4)
                            dve.wait_ge(consts_set, 5)
                            dve.tensor_copy(ident_r[:, :], ident[:, :]).then_inc(consts_cast, 1)
                            dve.tensor_copy(trit_r[:, :], prob_sum[:, 0, 0:P]).then_inc(consts_cast, 1)
                            dve.wait_ge(rms_in, 16)
                        elif e[0] == "xn":
                            t = e[1]
                            dve.wait_ge(rstd_done, t // 4 + 1)
                            dve.tensor_scalar(prob[:, t % 3, :], acc[:, t, :], rstd[:, t:t + 1], None, ALU.mult
                                              ).then_inc(xn_done, 1)
                        elif e[0] == "norm":
                            t = e[1]
                            dve.wait_ge(y_hi_done, t + 1)
                            dve.tensor_tensor(yt_lo[:, :, t * P:(t + 1) * P],
                                              x_bank(plan, e)[:, :].rearrange("p (k q) -> p k q", k=KC),
                                              yt_hi[:, :, t * P:(t + 1) * P].bitcast(F32), ALU.subtract
                                              ).then_inc(y_lo_done, 1)
                        elif e[0] == "mx":
                            _, b, s, h, c = e
                            n = b * CHUNKS + chunk_index(s, h, c)
                            bank = wait_x_full(dve, plan, g, e)
                            wait(dve, neg_max_done, g, 2 * NT, b * NT + s)
                            cols = row_chunks(s)[c][1] * P
                            if s >= 4 and c == 0:
                                dve.reduce_max(row_max[:, h:h + 1], bank[:, :], AX_X).then_inc(mx_done, 1)
                            else:
                                wait(dve, mx_done, g, 2 * CHUNKS, n - 1)
                                met(dve)
                                dve.tensor_tensor_reduce(out=junk[:, n % 2, 0:cols], in0=bank[:, 0:cols],
                                                         in1=mask[:, BANK - cols:BANK], scale=-1.0, scalar=3e38,
                                                         op0=ALU.add, op1=ALU.min,
                                                         accum_out=neg_max[:, h:h + 1]).then_inc(mx_done, 1)
                        elif e[0] == "mr":
                            _, b, s = e
                            wait(dve, mx_done, g, 2 * CHUNKS, b * CHUNKS + chunk_index(s, HG, 0))
                            wait(dve, shift_done, g, 2 * NT, b * NT + s)
                            if s >= 4:
                                dve.scalar_tensor_tensor(out=neg_max_r[:, :], in0=row_max[:, :], scalar=-1.0,
                                                         in1=neg_max[:, :], op0=ALU.mult, op1=ALU.min
                                                         ).then_inc(neg_max_done, 1)
                            else:
                                dve.tensor_copy(neg_max_r[:, :], neg_max[:, :]).then_inc(neg_max_done, 1)
                        elif e[0] == "w":
                            k, bank = e[1], x_bank(plan, e)
                            wait(dve, win_hi_done, g, 4, 4 + k + 1)
                            dve.scalar_tensor_tensor(out=win_lo[:, k, :], in0=bank[:, 0:WC], scalar=rms[:, k:k + 1],
                                                     in1=win_hi[:, k, :].bitcast(F32), op0=ALU.mult, op1=ALU.subtract
                                                     ).then_inc(win_done, 1)
                        elif e[0] == "wo":
                            k, bank = e[1], x_bank(plan, e)
                            wait(dve, wout_hi_done, g, 2, k + 1)
                            dve.tensor_tensor(wout_lo[:, k, :], bank[:, :], wout_hi[:, k, :].bitcast(F32),
                                              ALU.subtract).then_inc(wout_done, 1)
                        elif e[0] == "fw":
                            n, bank = e[1], x_bank(plan, e)
                            dve.wait_ge(ffn_in[0], 16 * (n + 1))
                            dve.wait_ge(ffn_in[1], 16 * (n + 1))
                            dve.tensor_scalar(raw[:, 2, :], raw[:, 0, :], TH_W, SC_W, ALU.is_gt, ALU.mult
                                              ).then_inc(tern_step, 1)
                            dve.tensor_scalar(raw[:, 0, :], raw[:, 0, :], -TH_W, SC_W, ALU.is_lt, ALU.mult
                                              ).then_inc(tern_step, 1)
                            dve.wait_ge(tern_step, 3 * n + 2)
                            dve.tensor_tensor(raw[:, 2, :], raw[:, 2, :], raw[:, 0, :], ALU.subtract
                                              ).then_inc(tern_step, 1)
                            dve.wait_ge(tern_step, 3 * n + 3)
                            dve.tensor_tensor(raw[:, 2, :], raw[:, 2, :], raw[:, 1, :], ALU.add).then_inc(ffn_w_done, 1)
                            dve.wait_ge(ffn_hi_done, n + 1)
                            dve.tensor_tensor(ffn_lo[:, :, n * P:(n + 1) * P],
                                              bank[:, :].rearrange("p (k q) -> p k q", k=KC),
                                              ffn_hi[:, :, n * P:(n + 1) * P].bitcast(F32), ALU.subtract
                                              ).then_inc(ffn_lo_done, 1)
                        elif e[0] == "qkv":
                            _, b, t = e
                            n = b * NT + t
                            bank = wait_x_full(dve, plan, g, e)
                            heads = bank[:, 0:QC + DH].rearrange("p (h d) -> p h d", d=DH)
                            wait(dve, stack_hi, g, 4 * NT, 2 * n)
                            dve.tensor_tensor(rope_a[:, :, :], heads,
                                              cos_sb[:, t:t + 1, :].to_broadcast([P, HG + 1, DH]), ALU.mult)
                            dve.tensor_tensor(
                                rope_b[:, :, :].rearrange("p h (a d) -> p h a d", a=2),
                                heads.rearrange("p h (a d) -> p h a d", a=2)[:, :, ::-1, :],
                                sin_sb[:, t:t + 1, :].to_broadcast([P, HG + 1, DH])
                                .rearrange("p h (a d) -> p h a d", a=2), ALU.mult).then_inc(roped_ab, 1)
                            wait(dve, pv_done, g, BODY, (b - 1) * UNITS)
                            dve.tensor_copy(v_sb[:, b % 2, t, 0:DH], bank[:, QC + DH:WC]).then_inc(v_hi_done, 1)
                            wait(dve, v_hi_done, g, 2 * NT, n + 1)
                            dve.tensor_tensor(v_sb[:, b % 2, t, DH:P], bank[:, QC + DH:WC],
                                              v_sb[:, b % 2, t, 0:DH].bitcast(F32), ALU.subtract).then_inc(v_done, 1)
                        elif e[0] == "oe":
                            _, b, s = e
                            kk = b * NT + s
                            wait(dve, o_low_done, g, 2 * NT, kk + 1)
                            wait(dve, o_t_done, g, 2 * NT, kk)
                            top = ot_ps[kk % 2][0:DH, :].rearrange("p (c a q) -> p a c q", c=2, a=2)
                            low = o_low[:, :].rearrange("p (c a q) -> p a c q", c=2, a=2)
                            dve.tensor_tensor(o_raw[0:DH, :, :], top[:, 0], low[:, 0], ALU.add)
                            dve.tensor_tensor(o_raw[DH:P, :, :], top[:, 1], low[:, 1], ALU.add).then_inc(o_raw_done, 1)
                        elif e[0] == "os":
                            _, b, s = e
                            bank = wait_x_full(dve, plan, g, e)
                            wait(dve, o_t_done, g, 2 * NT, b * NT + s)
                            dve.reciprocal(recip[:, :], bank[:, 0:HG]).then_inc(recip_done, 1)
                        elif e[0] == "ob":
                            _, b, s = e
                            kk = b * NT + s
                            bank = wait_x_full(dve, plan, g, e)
                            wait(dve, o_raw_done, g, 2 * NT, kk + 1)
                            wait(dve, o_lo_done, g, 2 * NT, kk)
                            dve.tensor_tensor(o_t[:, :, :], bank[:, 0:2 * P].rearrange("p (c q) -> p c q", c=2),
                                              o_raw[:, :, :], ALU.mult).then_inc(o_t_done, 1)
                        elif e[0] == "oh":
                            _, b, s = e
                            kk = b * NT + s
                            wait(dve, o_hi_done, g, 2 * NT, kk + 1)
                            dve.tensor_tensor(o_lo[:, :, :], o_t[:, :, :], o_hi[:, :, :].bitcast(F32), ALU.subtract
                                              ).then_inc(o_lo_done, 1)
                        elif e[0] == "op":
                            _, b, s = e
                            bank = wait_x_full(dve, plan, g, e)
                            tile = acc[:, (b * NT + s) % TT, :]
                            wait(dve, acc_done, g, 2 * NT, (b - 1) * NT + s)
                            if plan is opening:
                                dve.scalar_tensor_tensor(out=tile, in0=tile, scalar=2.0, in1=bank[:, :], op0=ALU.mult,
                                                         op1=ALU.add).then_inc(acc_done, 1)
                            else:
                                dve.tensor_tensor(tile, tile, bank[:, :], ALU.add).then_inc(acc_done, 1)

                if plan is opening:
                    dve.tensor_scalar(acc[:, TT - 1, :], acc[:, TT - 1, :], 2.0, None, ALU.mult).then_inc(doubled, 1)
                    dve.wait_ge(doubled, 1)
                for u in range(len(plan.ahead)):
                    events(plan.ahead[u])
                    if u < plan.units:
                        wait(dve, prob_hi_done, g, BODY, u + 1)
                        wait(dve, pv_done, g, BODY, u - 1)
                        dve.tensor_tensor(prob_lo[:, u % 2, :], prob[:, u % 3, :], prob_hi[:, u % 2, :].bitcast(F32),
                                          ALU.subtract).then_inc(prob_lo_done, 1)
                    events(plan.behind[u])

            over_bodies(dve, one)

            for k in LATE:
                if runs(k, TERN):
                    first_norm(k - TERN)
                if runs(k, OUT):
                    dve.wait_ge(ffn_done, k - OUT - NT + 1)
                    residual(k - OUT, ot_ps[(k - OUT) % 2])
                if runs(k, TERN):
                    below(k - TERN)
                if runs(k, OUT):
                    dve.wait_ge(x2_done, k - OUT + 1)
                    statistics(1, k - OUT)
                if runs(k, TERN):
                    ternary(k - TERN)
                if runs(k, OUT):
                    moments_of(1, k - OUT)
                if runs(k, LN):
                    dve.wait_ge(acc_done, LAST * TT + k - LN + 1)
                    statistics(0, k - LN)
                    moments_of(0, k - LN)

        @block.tensor
        def _(pe):
            pe.wait_ge(ident_in, 16)

            def turn_ternary(t, bank):
                pe.wait_ge(tern_done, t + 1)
                for c in range(KC):
                    mm = pe.transpose(bank[:, c * P:(c + 1) * P], tern_tile(t)[:, c * P:(c + 1) * P], ident[:, :])
                return mm

            def feed_forward(t, bank):
                pe.wait_ge(xq_done, t + 1)
                for c in range(KC):
                    for w in (ffn_hi, ffn_lo):
                        mm = pe.matmul(bank[:, :], xq_tile(t)[:, c, :], w[:, c, :], start=(c == 0 and w is ffn_hi),
                                       stop=(c == KC - 1 and w is ffn_lo))
                return mm

            def one(g, plan):
                def values(u):
                    b, s, j = unit_of(u)
                    k = b * NT + s
                    wait(pe, prob_hi_done, g, BODY, u + 1)
                    if j == 0:
                        wait(pe, o_raw_done, g, 2 * NT, k - 1)
                    values_t = v_sb[:, b % 2, j, :]
                    pe.matmul(ot_ps[k % 2][:, :], values_t, prob_hi[:, u % 2, :], start=(j == 0), stop=False)
                    wait(pe, prob_lo_done, g, BODY, u + 1)
                    pe.matmul(ot_ps[k % 2][:, :], values_t, prob_lo[:, u % 2, :], start=False, stop=(j == s)
                              ).then_inc(pv_done, 1)

                def events(some):
                    for e in some:
                        if e[0] in X_KINDS:
                            wait_x_free(pe, plan, g, e)
                            bank = x_bank(plan, e)
                        if e[0] == "tern":
                            turn_ternary(e[1], bank).then_inc(x_full, 1)
                        elif e[0] == "ffn":
                            if e[1] == 0:
                                pe.wait_ge(ffn_lo_done, KC)
                            feed_forward(e[1], bank).then_inc(x_full, 1)
                        elif e[0] == "norm":
                            t = e[1]
                            pe.wait_ge(xn_done, t + 1)
                            for k in range(KC):
                                mm = pe.transpose(bank[:, k * P:(k + 1) * P], prob[:, t % 3, k * P:(k + 1) * P],
                                                  ident[:, :])
                            mm.then_inc(x_full, 1)
                        elif e[0] == "mx":
                            _, b, s, h, c = e
                            n = b * CHUNKS + chunk_index(s, h, c)
                            t0, tiles = row_chunks(s)[c]
                            wait(pe, qt_done, g, 2 * NT, b * NT + s + 1)
                            wait(pe, kt_done, g, 2 * NT, b * NT + t0 + tiles)
                            pe.matmul(bank[:, 0:tiles * P], q_t[:, h, s * P:(s + 1) * P],
                                      k_t[:, b % 2, 0, t0 * P:(t0 + tiles) * P], start=True, stop=True
                                      ).then_inc(x_full, 1)
                        elif e[0] == "mr":
                            _, b, s = e
                            wait(pe, neg_max_done, g, 2 * NT, b * NT + s + 1)
                            if plan is first:
                                pe.wait_ge(consts_cast, 1)
                            for h in range(HG):
                                mm = pe.matmul(bank[0:1, h * P:(h + 1) * P], neg_max_r[:, h:h + 1], ident_r[:, :],
                                               start=True, stop=True)
                            mm.then_inc(x_full, 1)
                        elif e[0] == "w":
                            wait(pe, win_in, g, 48, 96)
                            for a in range(3):
                                mm = pe.transpose(bank[:, a * P:(a + 1) * P], raw[:, a, e[1] * P:(e[1] + 1) * P],
                                                  ident[:, :])
                            mm.then_inc(x_full, 1)
                        elif e[0] == "wo":
                            wait(pe, wout_in, g, 16, 16)
                            for a in range(KC):
                                mm = pe.transpose(bank[:, a * P:(a + 1) * P], wout_raw[:, a, e[1] * P:(e[1] + 1) * P],
                                                  ident[:, :])
                            mm.then_inc(x_full, 1)
                        elif e[0] == "qkv":
                            _, b, t = e
                            wait(pe, win_done, g, 4, 8 if b == 2 else 4)
                            tile = (b % 2) * NT + t
                            if plan is first:
                                pe.wait_ge(y_lo_done, tile + 1)
                            for k in range(KC):
                                for n, (y, w) in enumerate(((yt_hi, win_hi), (yt_hi, win_lo), (yt_lo, win_hi))):
                                    mm = pe.matmul(bank[:, 0:WC], y[:, k, tile * P:(tile + 1) * P], w[:, k, :],
                                                   start=(k == 0 and n == 0), stop=(k == KC - 1 and n == 2))
                            mm.then_inc(x_full, 1)
                        elif e[0] == "fw":
                            pe.wait_ge(ffn_w_done, e[1] + 1)
                            for a in range(KC):
                                mm = pe.transpose(bank[:, a * P:(a + 1) * P], raw[:, 2, a * P:(a + 1) * P],
                                                  ident[:, :])
                            mm.then_inc(x_full, 1)
                        elif e[0] in ("qt", "kt"):
                            _, b, t = e
                            wait(pe, stack_done, g, 4 * NT, 2 * (b * NT + t + 1))
                            for n, a in enumerate(range(HG) if e[0] == "qt" else (HG, HG + 1)):
                                mm = pe.transpose(bank[:, n * P:(n + 1) * P], stack[:, a, :].bitcast(F32), ident[:, :])
                            mm.then_inc(x_full, 1)
                        elif e[0] == "os":
                            _, b, s = e
                            wait(pe, sum_done, g, BODY, b * UNITS + first_unit(s + 1))
                            for h in range(HG):
                                mm = pe.matmul(bank[:, h:h + 1], prob_sum[:, (b * NT + s) % 2, h * P:(h + 1) * P],
                                               ones[:, :], start=True, stop=True)
                            mm.then_inc(x_full, 1)
                        elif e[0] == "ob":
                            _, b, s = e
                            wait(pe, recip_done, g, 2 * NT, b * NT + s + 1)
                            for h in range(HG):
                                c, a = divmod(h, 2)
                                mm = pe.matmul(bank[a * DH:(a + 1) * DH, c * P:(c + 1) * P],
                                               recip[:, h:h + 1].to_broadcast([P, DH]), ident[:, :],
                                               start=True, stop=True)
                            mm.then_inc(x_full, 1)
                        elif e[0] == "op":
                            _, b, s = e
                            wait(pe, wout_done, g, 2, 2 if b >= 0 else 0)
                            wait(pe, o_hi_done, g, 2 * NT, b * NT + s + 1)
                            wait(pe, o_lo_done, g, 2 * NT, b * NT + s + 1)
                            for c in range(2):
                                for n, (o, w) in enumerate(((o_hi, wout_hi), (o_hi, wout_lo), (o_lo, wout_hi))):
                                    mm = pe.matmul(bank[:, :], o[:, c, :], w[:, c, :], start=(c == 0 and n == 0),
                                                   stop=(c == 1 and n == 2))
                            mm.then_inc(x_full, 1)

                if plan is opening:
                    pe.wait_ge(y_lo_done, TT)
                    pe.wait_ge(consts_cast, 2)
                    pe.wait_ge(consts_set, 5)
                for u in range(len(plan.ahead)):
                    if u < plan.units:
                        b, s, j = unit_of(u)
                        k = (b * NT + s) % 2
                        if j == 0:
                            wait(pe, q_shift_in[k], g, 16 * NT, 16 * ((b * NT + s) // 2 + 1))
                            wait(pe, shift_done, g, 2 * NT, b * NT + s + 1)
                            wait(pe, v_done, g, 2 * NT, b * NT + s + 1)
                        wait(pe, prob_hi_done, g, BODY, u - 1)
                        bank = st_ps[u % 2]
                        keys = k_t[:, b, :, j * P:(j + 1) * P]
                        pe.matmul(bank[:, :], keys[:, 0], q_tile(s), start=True, stop=False)
                        mm = pe.matmul(bank[:, :], keys[0:DH + 1, 1], q_shift[0:DH + 1, k, :, :], start=False,
                                       stop=(j < s))
                        if j == s:
                            mm = pe.matmul(bank[:, :], ident_r[:, :],
                                           trit_r[:, :].unsqueeze(1).to_broadcast([P, HG, P]), start=False, stop=True)
                        mm.then_inc(st_done, 1)
                    events(plan.ahead[u])
                    events(plan.behind[u])
                    if 0 < u <= plan.units or u == 0 and plan in (body, final):
                        values(u - 1)

            over_bodies(pe, one)

            for k in LATE:
                if runs(k, FFN):
                    t = k - FFN
                    feed_forward(t, ot_ps[t % 2]).then_inc(ffn_done, 1)
                if runs(k, TERN):
                    t = k - TERN
                    if t >= NT + 2:
                        pe.wait_ge(xq_done, t - 1)
                    turn_ternary(t, x_ps[t % 2]).then_inc(tern_t_full, 1)


_INS = ["L0_attn_x", "L0_attn_w_in", "L0_attn_w_out", "L0_attn_rms_w", "L0_ffn_weight", "L0_ffn_rram_variation"]


def shape_constants(seq):
    import numpy as np

    f = np.float32
    exponent = np.arange(0, DH, 2, dtype=f) / f(DH)
    inv_freq = f(1) / (ROPE_THETA ** exponent.astype(np.float64)).astype(f)
    angle = (np.arange(seq, dtype=f)[:, None] * inv_freq[None, :]).astype(np.float64)
    cos, sin = np.cos(angle).astype(f), np.sin(angle).astype(f)
    later = np.triu(np.full((P, P), MASKED, f), 1)
    return {
        "cos_dram": np.concatenate([cos, cos], 1), "sin_dram": np.concatenate([-sin, sin], 1),
        "ident_dram": np.eye(P, dtype=f), "tri_dram": later, "trit_dram": np.ascontiguousarray(later.T),
    }


def kernel(**inputs):
    import numpy as np
    import concourse.bacc as bacc
    from concourse.bass_utils import run_bass_kernel_spmd as run

    nc = bacc.Bacc("TRN2", target_bir_lowering=False, num_devices=1)
    arrays = {name: np.ascontiguousarray(inputs[name]) for name in _INS}
    shape = arrays["L0_attn_x"].shape
    arrays["L0_attn_rms_w"] = np.ascontiguousarray(arrays["L0_attn_rms_w"].reshape(-1, P).T)
    arrays.update(shape_constants(shape[1]))
    args = [nc.dram_tensor(n, a.shape, mybir.dt.from_np(a.dtype), kind="ExternalInput").ap() for n, a in arrays.items()]
    args.append(nc.dram_tensor("out", shape, F32, kind="ExternalOutput").ap())
    seq_block(nc, *args)
    return run(nc, [arrays], core_ids=[0]).results[0]["out"]
```
